# Optimizing a Trainium2 kernel written in Bass

```python
import numpy as np
import jax
import jax.numpy as jnp

def _softmax(x, axis=-1):
    return jax.nn.softmax(x, axis=axis)

def _gelu(x):
    return jax.nn.gelu(x, approximate=True)

def _silu(x):
    return jax.nn.silu(x)

def _sigmoid(x):
    return jax.nn.sigmoid(x)

def _layernorm(x, axis=-1, eps=1e-05):
    m = jnp.mean(x, axis=axis, keepdims=True)
    v = jnp.var(x, axis=axis, keepdims=True)
    return (x - m) / jnp.sqrt(v + eps)

def _scatter_add(tgt, idx, src, axis=0):
    return tgt.at[idx].add(src)

def _segment_sum(src, seg, n):
    return jax.ops.segment_sum(src, seg, n)
kernel_name = 'mk_xattn_ffn_d2_seqx_r8_e82ec3'

def setup_inputs(seed: int=0):
    np.random.seed(seed)
    _w = jnp.asarray

    def _rec_inputs():
        import jax
        import jax.numpy as jnp
        _rk = jax.random.key(seed)
        x = 7.22e-05 + 1 * jax.random.normal(jax.random.fold_in(_rk, 1), (32, 128, 128), jnp.float32)
        _lenS = 128 - jax.random.randint(jax.random.fold_in(_rk, 7), (32,), 0, max(1, 128 // 4) + 1, jnp.int32)
        _lenS2 = 128 - jax.random.randint(jax.random.fold_in(_rk, 8), (32,), 0, max(1, 128 // 4) + 1, jnp.int32)
        _ctx_1024P = jax.random.normal(jax.random.fold_in(_rk, 11), (32, 16, 128), jnp.float32)
        _ctx_1024c = jax.random.dirichlet(jax.random.fold_in(_rk, 511), 0.3 * jnp.ones((16,), jnp.float32), (32, 128))
        _ctx_1024t = jnp.einsum('bsk,bkd->bsd', _ctx_1024c, _ctx_1024P)
        _ctx_1024t = _ctx_1024t * jax.lax.rsqrt(jnp.mean(jnp.square(_ctx_1024t)) + 1e-12) * 0.953939
        ctx_1024 = 4.13588e-05 + 0.999923 * (_ctx_1024t + 0.3 * jax.random.normal(jax.random.fold_in(_rk, 611), (32, 128, 128), jnp.float32))
        _validS = jnp.arange(128)[None, :] < _lenS[:, None]
        _validS2 = jnp.arange(128)[None, :] < _lenS2[:, None]
        _causal = jnp.tril(jnp.ones((128, 128), dtype=bool))
        mask_BxS2_bf1 = jnp.ones((32, 128), dtype=bool)
        return (x, ctx_1024, mask_BxS2_bf1)
    x, ctx_1024, mask_BxS2_bf1 = _rec_inputs()

    def _L0_xattn_setup():
        import jax, jax.numpy as jnp
        import numpy as np
        D_MODEL = 128
        NHEAD = 16
        HEAD_DIM = D_MODEL // NHEAD
        key = jax.random.key(seed)
        ks = jax.random.split(key, 11)
        B, S, D = (4, 256, D_MODEL)
        scale = 1.0 / np.sqrt(D)
        inp = {'q': jax.random.normal(ks[0], (B, S, D), jnp.float32), 'k': jax.random.normal(ks[1], (B, S, D), jnp.float32), 'v': jax.random.normal(ks[2], (B, S, D), jnp.float32), 'Wq': jax.random.normal(ks[3], (D, D), jnp.float32) * scale, 'bq': jnp.zeros((D,), jnp.float32), 'Wk': jax.random.normal(ks[4], (D, D), jnp.float32) * scale, 'bk': jnp.zeros((D,), jnp.float32), 'Wv': jax.random.normal(ks[5], (D, D), jnp.float32) * scale, 'bv': jnp.zeros((D,), jnp.float32), 'Wo': jax.random.normal(ks[6], (D, D), jnp.float32) * scale, 'bo': jnp.zeros((D,), jnp.float32)}
        return inp
    _L0_xattn_all = _L0_xattn_setup()
    _L0_xattn_in = {k: v for k, v in _L0_xattn_all.items() if k in ('Wq', 'bq', 'Wk', 'bk', 'Wv', 'bv', 'Wo', 'bo')}
    del _L0_xattn_all

    def _L0_ffn_setup():
        import jax, jax.numpy as jnp
        import numpy as np
        B, S, D, E, F = (4, 256, 128, 8, 512)
        MIN_CAPACITY = 4

        def _make_waff():
            g = D // E
            scale = E / D
            w = np.zeros((E, D), np.float32)
            for i in range(E):
                w[i, i * g:(i + 1) * g] = scale
            return jnp.asarray(w)
        key = jax.random.key(seed)
        ks = jax.random.split(key, 6)
        inputs = jax.random.normal(ks[0], (B, S, D), dtype=jnp.float32)
        W1 = jax.random.normal(ks[1], (E, D, F), dtype=jnp.float32) * (1.0 / np.sqrt(D))
        b1 = jnp.zeros((E, F), dtype=jnp.float32)
        W2 = jax.random.normal(ks[2], (E, F, D), dtype=jnp.float32) * (1.0 / np.sqrt(F))
        b2 = jnp.zeros((E, D), dtype=jnp.float32)
        return {'inputs': inputs, 'waff': _make_waff(), 'W1': W1, 'b1': b1, 'W2': W2, 'b2': b2, 'affinity_threshold': jnp.float32(0.5)}
    _L0_ffn_all = _L0_ffn_setup()
    _L0_ffn_in = {k: v for k, v in _L0_ffn_all.items() if k in ('waff', 'W1', 'b1', 'W2', 'b2', 'affinity_threshold')}
    del _L0_ffn_all

    def _L1_xattn_setup():
        import jax, jax.numpy as jnp
        import numpy as np
        EPS = 1e-06
        NUM_HEADS = 16
        DIM_HEADS = 64

        def _ln(x, scale, bias):
            mu = jnp.mean(x, axis=-1, keepdims=True)
            var = jnp.mean(jnp.square(x - mu), axis=-1, keepdims=True)
            return (x - mu) * jax.lax.rsqrt(var + EPS) * scale + bias
        key = jax.random.key(seed)
        ks = jax.random.split(key, 8)
        b, n, m, dim, ctx_dim = (8, 512, 32, 128, 128)
        inner = NUM_HEADS * DIM_HEADS
        x = jax.random.normal(ks[0], (b, n, dim), dtype=jnp.float32)
        context = jax.random.normal(ks[1], (b, m, ctx_dim), dtype=jnp.float32)
        mask = jnp.ones((b, m), dtype=bool)
        Wq = jax.random.normal(ks[2], (dim, inner), dtype=jnp.float32) / np.sqrt(dim)
        Wkv = jax.random.normal(ks[3], (ctx_dim, 2 * inner), dtype=jnp.float32) / np.sqrt(ctx_dim)
        null_kv = jax.random.normal(ks[4], (2, DIM_HEADS), dtype=jnp.float32)
        Wo = jax.random.normal(ks[5], (inner, dim), dtype=jnp.float32) / np.sqrt(inner)
        return {'x': x, 'context': context, 'mask': mask, 'ln1_s': jnp.ones((dim,), jnp.float32), 'ln1_b': jnp.zeros((dim,), jnp.float32), 'lnc_s': jnp.ones((ctx_dim,), jnp.float32), 'lnc_b': jnp.zeros((ctx_dim,), jnp.float32), 'Wq': Wq, 'Wkv': Wkv, 'null_kv': null_kv, 'Wo': Wo, 'lno_s': jnp.ones((dim,), jnp.float32), 'lno_b': jnp.zeros((dim,), jnp.float32)}
    _L1_xattn_all = _L1_xattn_setup()
    _L1_xattn_in = {k: v for k, v in _L1_xattn_all.items() if k in ('ln1_s', 'ln1_b', 'lnc_s', 'lnc_b', 'Wq', 'Wkv', 'null_kv', 'Wo', 'lno_s', 'lno_b')}
    del _L1_xattn_all

    def _L1_ffn_setup():
        import jax, jax.numpy as jnp
        import numpy as np
        HIDDEN = 128
        INNER = 512

        def _weight_quant(w):
            scale = 1.0 / jnp.clip(jnp.mean(jnp.abs(w)), 1e-05)
            wq = jnp.clip(jnp.round(w * scale), -1.0, 1.0) / scale
            return w + jax.lax.stop_gradient(wq - w)

        def _act_quant(x):
            scale = 127.0 / jnp.clip(jnp.max(jnp.abs(x), axis=-1, keepdims=True), 1e-05)
            xq = jnp.clip(jnp.round(x * scale), -128.0, 127.0) / scale
            return x + jax.lax.stop_gradient(xq - x)

        def _bitlinear(x, w):
            return jnp.einsum('bsi,oi->bso', _act_quant(x), _weight_quant(w))
        key = jax.random.key(seed)
        k0, k1, k2, k3 = jax.random.split(key, 4)
        x = jax.random.normal(k0, (4, 256, HIDDEN), dtype=jnp.float32)
        w_gate = jax.random.normal(k1, (INNER, HIDDEN), dtype=jnp.float32) / np.sqrt(HIDDEN)
        w_up = jax.random.normal(k2, (INNER, HIDDEN), dtype=jnp.float32) / np.sqrt(HIDDEN)
        w_down = jax.random.normal(k3, (HIDDEN, INNER), dtype=jnp.float32) / np.sqrt(INNER)
        return {'x': x, 'w_gate': w_gate, 'w_up': w_up, 'w_down': w_down}
    _L1_ffn_all = _L1_ffn_setup()
    _L1_ffn_in = {k: v for k, v in _L1_ffn_all.items() if k in ('w_gate', 'w_up', 'w_down')}
    del _L1_ffn_all
    return {'x': x, 'ctx_1024': ctx_1024, 'mask_BxS2_bf1': mask_BxS2_bf1, 'L0_xattn_Wq': _L0_xattn_in['Wq'], 'L0_xattn_bq': _L0_xattn_in['bq'], 'L0_xattn_Wk': _L0_xattn_in['Wk'], 'L0_xattn_bk': _L0_xattn_in['bk'], 'L0_xattn_Wv': _L0_xattn_in['Wv'], 'L0_xattn_bv': _L0_xattn_in['bv'], 'L0_xattn_Wo': _L0_xattn_in['Wo'], 'L0_xattn_bo': _L0_xattn_in['bo'], 'L0_ffn_waff': _L0_ffn_in['waff'], 'L0_ffn_W1': _L0_ffn_in['W1'], 'L0_ffn_b1': _L0_ffn_in['b1'], 'L0_ffn_W2': _L0_ffn_in['W2'], 'L0_ffn_b2': _L0_ffn_in['b2'], 'L0_ffn_affinity_threshold': _L0_ffn_in['affinity_threshold'], 'L1_xattn_ln1_s': _L1_xattn_in['ln1_s'], 'L1_xattn_ln1_b': _L1_xattn_in['ln1_b'], 'L1_xattn_lnc_s': _L1_xattn_in['lnc_s'], 'L1_xattn_lnc_b': _L1_xattn_in['lnc_b'], 'L1_xattn_Wq': _L1_xattn_in['Wq'], 'L1_xattn_Wkv': _L1_xattn_in['Wkv'], 'L1_xattn_null_kv': _L1_xattn_in['null_kv'], 'L1_xattn_Wo': _L1_xattn_in['Wo'], 'L1_xattn_lno_s': _L1_xattn_in['lno_s'], 'L1_xattn_lno_b': _L1_xattn_in['lno_b'], 'L1_ffn_w_gate': _L1_ffn_in['w_gate'], 'L1_ffn_w_up': _L1_ffn_in['w_up'], 'L1_ffn_w_down': _L1_ffn_in['w_down']}

def reference(x, ctx_1024, mask_BxS2_bf1, L0_xattn_Wq, L0_xattn_bq, L0_xattn_Wk, L0_xattn_bk, L0_xattn_Wv, L0_xattn_bv, L0_xattn_Wo, L0_xattn_bo, L0_ffn_waff, L0_ffn_W1, L0_ffn_b1, L0_ffn_W2, L0_ffn_b2, L0_ffn_affinity_threshold, L1_xattn_ln1_s, L1_xattn_ln1_b, L1_xattn_lnc_s, L1_xattn_lnc_b, L1_xattn_Wq, L1_xattn_Wkv, L1_xattn_null_kv, L1_xattn_Wo, L1_xattn_lno_s, L1_xattn_lno_b, L1_ffn_w_gate, L1_ffn_w_up, L1_ffn_w_down):
    import jax
    import jax.numpy as jnp

    def _L0_xattn_ref(q, k, v, Wq, bq, Wk, bk, Wv, bv, Wo, bo):
        import jax, jax.numpy as jnp
        import numpy as np
        D_MODEL = 128
        NHEAD = 16
        HEAD_DIM = D_MODEL // NHEAD
        B, S, D = q.shape
        H, Hd = (NHEAD, HEAD_DIM)
        qh = (q @ Wq.T + bq).reshape(B, S, H, Hd).transpose(0, 2, 1, 3)
        kh = (k @ Wk.T + bk).reshape(B, S, H, Hd).transpose(0, 2, 1, 3)
        vh = (v @ Wv.T + bv).reshape(B, S, H, Hd).transpose(0, 2, 1, 3)
        scores = jnp.einsum('bhqd,bhkd->bhqk', qh, kh) / jnp.sqrt(jnp.float32(Hd))
        attn = jax.nn.softmax(scores, axis=-1)
        out = jnp.einsum('bhqk,bhkd->bhqd', attn, vh)
        out = out.transpose(0, 2, 1, 3).reshape(B, S, D)
        return out @ Wo.T + bo

    def _L0_ffn_ref(inputs, waff, W1, b1, W2, b2, affinity_threshold):
        import jax, jax.numpy as jnp
        import numpy as np
        B, S, D, E, F = (4, 256, 128, 8, 512)
        MIN_CAPACITY = 4

        def _make_waff():
            g = D // E
            scale = E / D
            w = np.zeros((E, D), np.float32)
            for i in range(E):
                w[i, i * g:(i + 1) * g] = scale
            return jnp.asarray(w)
        num = jnp.einsum('bsd,ed->bse', inputs, waff)
        x_norm = jnp.linalg.norm(inputs, axis=-1, keepdims=True)
        w_norm = jnp.linalg.norm(waff, axis=-1)
        aff = num / (x_norm * w_norm[None, None, :] + 1e-09)
        router_probs = jax.nn.softmax(aff, axis=-1)
        cap = jnp.floor(S * jax.nn.sigmoid(aff.mean() - affinity_threshold)).astype(jnp.int32)
        cap = jnp.minimum(jnp.maximum(cap, MIN_CAPACITY), S)
        tcr = jax.nn.one_hot(jnp.argmax(router_probs, axis=-1), E, dtype=inputs.dtype)
        order = jnp.argsort(-aff, axis=1)
        ranks = jnp.argsort(order, axis=1)
        ecr = (ranks < cap).astype(inputs.dtype)
        dispatch = tcr * ecr
        masks = jnp.moveaxis(dispatch, -1, 0)

        def body(acc, expert):
            W1e, b1e, W2e, b2e, me = expert
            xi = inputs * me[..., None]
            h = jax.nn.gelu(xi @ W1e + b1e, approximate=False)
            return (acc + (h @ W2e + b2e), None)
        out, _ = jax.lax.scan(body, jnp.zeros_like(inputs), (W1, b1, W2, b2, masks))
        return out

    def _L1_xattn_ref(x, context, mask, ln1_s, ln1_b, lnc_s, lnc_b, Wq, Wkv, null_kv, Wo, lno_s, lno_b):
        import jax, jax.numpy as jnp
        import numpy as np
        EPS = 1e-06
        NUM_HEADS = 16
        DIM_HEADS = 64

        def _ln(x, scale, bias):
            mu = jnp.mean(x, axis=-1, keepdims=True)
            var = jnp.mean(jnp.square(x - mu), axis=-1, keepdims=True)
            return (x - mu) * jax.lax.rsqrt(var + EPS) * scale + bias
        b, n, _ = x.shape
        h, d = (NUM_HEADS, DIM_HEADS)
        scale = h ** (-0.5)
        xn = _ln(x, ln1_s, ln1_b)
        cn = _ln(context, lnc_s, lnc_b)
        q = xn @ Wq
        kv = cn @ Wkv
        k, v = jnp.split(kv, 2, axis=-1)

        def to_heads(t):
            return t.reshape(t.shape[0], t.shape[1], h, d).transpose(0, 2, 1, 3)
        q, k, v = (to_heads(q), to_heads(k), to_heads(v))
        nk = jnp.broadcast_to(null_kv[0], (b, h, 1, d))
        nv = jnp.broadcast_to(null_kv[1], (b, h, 1, d))
        k = jnp.concatenate((nk, k), axis=2)
        v = jnp.concatenate((nv, v), axis=2)
        sim = jnp.einsum('bhid,bhjd->bhij', q * scale, k)
        mfull = jnp.pad(mask, ((0, 0), (1, 0)), constant_values=True)[:, None, None, :]
        max_neg = -jnp.finfo(sim.dtype).max
        sim = jnp.where(mfull, sim, max_neg)
        attn = jax.nn.softmax(sim, axis=-1)
        out = jnp.einsum('bhij,bhjd->bhid', attn, v)
        out = out.transpose(0, 2, 1, 3).reshape(b, n, h * d)
        out = out @ Wo
        return _ln(out, lno_s, lno_b)

    def _L1_ffn_ref(x, w_gate, w_up, w_down):
        import jax, jax.numpy as jnp
        import numpy as np
        HIDDEN = 128
        INNER = 512

        def _weight_quant(w):
            scale = 1.0 / jnp.clip(jnp.mean(jnp.abs(w)), 1e-05)
            wq = jnp.clip(jnp.round(w * scale), -1.0, 1.0) / scale
            return w + jax.lax.stop_gradient(wq - w)

        def _act_quant(x):
            scale = 127.0 / jnp.clip(jnp.max(jnp.abs(x), axis=-1, keepdims=True), 1e-05)
            xq = jnp.clip(jnp.round(x * scale), -128.0, 127.0) / scale
            return x + jax.lax.stop_gradient(xq - x)

        def _bitlinear(x, w):
            return jnp.einsum('bsi,oi->bso', _act_quant(x), _weight_quant(w))
        gate = jax.nn.silu(_bitlinear(x, w_gate))
        up = _bitlinear(x, w_up)
        return _bitlinear(gate * up, w_down)
    x = x + _L0_xattn_ref(_layernorm(x, axis=-1), ctx_1024, ctx_1024, L0_xattn_Wq, L0_xattn_bq, L0_xattn_Wk, L0_xattn_bk, L0_xattn_Wv, L0_xattn_bv, L0_xattn_Wo, L0_xattn_bo)
    x = x + _L0_ffn_ref(_layernorm(x, axis=-1), L0_ffn_waff, L0_ffn_W1, L0_ffn_b1, L0_ffn_W2, L0_ffn_b2, L0_ffn_affinity_threshold)
    x = x + _L1_xattn_ref(_layernorm(x, axis=-1), ctx_1024, mask_BxS2_bf1, L1_xattn_ln1_s, L1_xattn_ln1_b, L1_xattn_lnc_s, L1_xattn_lnc_b, L1_xattn_Wq, L1_xattn_Wkv, L1_xattn_null_kv, L1_xattn_Wo, L1_xattn_lno_s, L1_xattn_lno_b)
    x = x + _L1_ffn_ref(_layernorm(x, axis=-1), L1_ffn_w_gate, L1_ffn_w_up, L1_ffn_w_down)
    return x

_drawn_inputs = setup_inputs


def setup_inputs(seed=0):
    import zlib

    import numpy as np

    out = dict(_drawn_inputs(seed))
    spreads = {'L0_xattn_bq': (0.0, 0.1),
     'L0_xattn_bk': (0.0, 0.1),
     'L0_xattn_bv': (0.0, 0.1),
     'L0_xattn_bo': (0.0, 0.1),
     'L0_ffn_b1': (0.0, 0.1),
     'L0_ffn_b2': (0.0, 0.1),
     'L1_xattn_ln1_s': (1.0, 0.2),
     'L1_xattn_ln1_b': (0.0, 0.1),
     'L1_xattn_lnc_s': (1.0, 0.2),
     'L1_xattn_lnc_b': (0.0, 0.1),
     'L1_xattn_lno_s': (1.0, 0.2),
     'L1_xattn_lno_b': (0.0, 0.1)}
    factors = {}
    for name, (base, spread) in spreads.items():
        noise = np.random.default_rng([zlib.crc32(name.encode()), seed]).standard_normal(out[name].shape)
        drawn = base * np.exp(spread * noise) if base else spread * noise
        out[name] = jnp.asarray(drawn.astype(out[name].dtype))
    for name, factor in factors.items():
        out[name] = (out[name] * factor).astype(out[name].dtype)
    return out
```

```python
from contextlib import ExitStack

import concourse.bass as bass
from concourse import mybir

ALU = mybir.AluOpType
ACT = mybir.ActivationFunctionType
BF16 = mybir.dt.bfloat16
F32 = mybir.dt.float32
I32 = mybir.dt.int32
U32 = mybir.dt.uint32
AX_X = mybir.AxisListType.X

P = 128
EPS_BLOCK = 1e-5
EPS_L1 = 1e-6


def wait(eng, sem, value):
    if isinstance(value, int) and value <= 0:
        return
    eng.wait_ge(sem, value)


def wait_apart(eng, consts, *waits):
    values = [v if isinstance(v, int) else eng.to_reg(v) for _, v in waits]
    eng.wait_ge(consts["ready"], consts["n_ready"])
    for (sem, _), value in zip(waits, values):
        wait(eng, sem, value)


def over_pairs(eng, n, step, between=None, tail=2):
    for b in (0, 1):
        step(b, b)
    if between is not None:
        between()
    with eng.Fori(1, (n - tail) // 2) as i:
        for s in range(2):
            step(2 * i + s, s)
    for b in range(n - tail, n):
        step(b, b % 2)


def known(b, value):
    return isinstance(b, int) and b == value


def at(t, b):
    if isinstance(b, int):
        return t[:, b, :]
    return t[:, bass.ds(b, 1), :].rearrange("p a d -> p (a d)")


def row(t, b):
    if isinstance(b, int):
        return t[b]
    return t[bass.ds(b, 1), :, :].rearrange("a p d -> p (a d)")


def lead(t):
    return t.bitcast(BF16)[:, 1::2]


def self_attention_block(nc, ctx, space, consts, x, ctxT, w, x_res, mv_out, psum):
    B, S, D = x.shape
    H = 16
    HD = D // H
    Q4 = 4
    SCALE = float(HD) ** -0.5

    def sb(name, shape, dt=F32):
        return space.enter_context(nc.sbuf_tensor(name, shape, dt))

    def sem(name):
        return ctx.enter_context(nc.semaphore(name))

    negI, ident, mask, minus_half = consts["negI"], consts["ident"], consts["mask"], consts["minus_half"]
    cst = consts["ready"]
    wq, wk, wv, wo = (sb(f"l0_w{n}", [P, D]) for n in "qkvo")
    bq, bk = sb("l0_bq", [P, 1]), sb("l0_bk", [P, 1])
    bv_row, bo_row = sb("l0_bv", [P, D]), sb("l0_bo", [P, D])
    cT = sb("l0_cT", [P, 2, S])
    bn = sb("l0_bn", [P, 2, 6])
    mv = sb("l0_mv", [P, 2, 2])
    rs = sb("l0_rs", [P, 2, 2])
    bn2, ag2 = sb("l0_bn2", [P, 2, 6]), sb("l0_ag2", [P, 2, 2])
    xb = sb("l0_xb", [P, 2, D])
    xn = sb("l0_xn", [P, 2, D])
    xT = sb("l0_xT", [P, 2, S])
    qz = sb("l0_qz", [P, 2, H, S])
    kT = sb("l0_kT", [P, 2, S])
    v = sb("l0_v", [P, 2, H, 32])
    mx = sb("l0_mx", [P, 2, H], BF16)
    pT = sb("l0_pT", [P, 2, Q4 * S])
    oev = sb("l0_oev", [P, 2, Q4 * S])
    rden = sb("l0_rden", [P, H])
    on = sb("l0_on", [P, D])
    oT = sb("l0_oT", [P, S])

    w_in = sem("l0_w_in")
    ones_set = sem("l0_ones_set")
    ld = [sem(f"l0_ld{s}") for s in range(2)]
    bn_done, mv_done, rv_done, rs_done = sem("l0_bn_done"), sem("l0_mv_done"), sem("l0_rv_done"), sem("l0_rs_done")
    xb_ready, xn_ready, xT_ready = sem("l0_xb_ready"), sem("l0_xn_ready"), sem("l0_xT_ready")
    xt_done, qkv_done = sem("l0_xt_done"), sem("l0_qkv_done")
    qz_ready, kT_ready, v_ready = sem("l0_qz_ready"), sem("l0_kT_ready"), sem("l0_v_ready")
    max_done, mx_ready = sem("l0_max_done"), sem("l0_mx_ready")
    t_done, exp_ready, pv_done = sem("l0_t_done"), sem("l0_exp_ready"), sem("l0_pv_done")
    oev_ready, tr_done, rden_ready, on_ready = sem("l0_oev_ready"), sem("l0_tr_done"), sem("l0_rden"), sem("l0_on")
    ot_done, oT_ready, wo_done = sem("l0_ot_done"), sem("l0_oT_ready"), sem("l0_wo_done")
    x1_ready, bn2_done, mv2_done = sem("l0_x1_ready"), sem("l0_bn2_done"), sem("l0_mv2_done")
    ag2_done = sem("l0_ag2_done")

    actp = psum[:, 0, :]
    dvep = psum[:, 1, :]
    maxp = [psum[:, 2 + s, :] for s in range(2)]
    tp = [psum[:, 4 + s, :] for s in range(2)]
    pv = psum[:, 6, :]
    outp = psum[:, 7, :]
    N_W = 8 * 16

    def sync_part(sp, after_first_loads):
        sp.dma_start(wq[:], w["Wq"]).then_inc(w_in, 16)
        sp.dma_start(wk[:], w["Wk"]).then_inc(w_in, 16)
        sp.dma_start(wv[:], w["Wv"]).then_inc(w_in, 16)
        sp.dma_start(wo[:], w["Wo"]).then_inc(w_in, 16)
        sp.dma_start(bq[:], w["bq"].rearrange("(d a) -> d a", a=1)).then_inc(w_in, 16)
        sp.dma_start(bk[:], w["bk"].rearrange("(d a) -> d a", a=1)).then_inc(w_in, 16)
        sp.dma_start(bv_row[:], w["bv"].partition_broadcast(P)).then_inc(w_in, 16)
        sp.dma_start(bo_row[:], w["bo"].partition_broadcast(P)).then_inc(w_in, 16)

        def step(b, s):
            wait(sp, qkv_done, b - 1)
            sp.dma_start(at(x_res, b), row(x, b)).then_inc(ld[s], 16)
            sp.dma_start(cT[:, s, :], row(ctxT, b)).then_inc(ld[s], 16)

        over_pairs(sp, B, step, after_first_loads)

    def loaded(eng, b, s):
        eng.wait_ge(ld[s], 32 * (b // 2 + 1) if isinstance(b, int) else (b - s) * 16 + 32)

    def pool_part(g):
        nc.gpsimd.memset(v[:, :, :, HD:], 1.0).then_inc(ones_set, 1)
        g.wait_ge(w_in, N_W)

        def rsqrt(b, s):
            wait_apart(g, consts, (mv_done, b + 1), (xn_ready, b - 1))
            nc.gpsimd.tensor_scalar_add(rs[:, s, 0:1], mv[:, s, 1:2], EPS_BLOCK).then_inc(rv_done, 1)
            g.wait_ge(rv_done, b + 1)
            nc.gpsimd.tensor_tensor(rs[:, s, 1:2], rs[:, s, 0:1], minus_half[:, 0:1], ALU.pow).then_inc(rs_done, 1)

        def x_plus(b, s):
            loaded(g, b, s)
            wait(g, x1_ready, b - 1)
            nc.gpsimd.tensor_tensor(xb[:, s, :], at(x_res, b), bo_row[:], ALU.add).then_inc(xb_ready, 1)

        def step(b, s):
            if not known(b, B - 1):
                rsqrt(b + 1, 1 - s)
            x_plus(b, s)

        rsqrt(0, 0)
        over_pairs(g, B, step)

    def tensor_part(pe):
        pe.wait_ge(cst, consts["n_ready"])
        pe.wait_ge(w_in, N_W)

        def x_transpose(b, s):
            pe.wait_ge(xn_ready, b + 1)
            wait(pe, kT_ready, b)
            nc.tensor.transpose(actp[:, 0:S], xn[:, s, :], ident[:]).then_inc(xt_done, 1)

        def projections(b, s):
            pe.wait_ge(xT_ready, b + 1)
            loaded(pe, b, s)
            wait(pe, qz_ready, b)
            wait(pe, v_ready, b)
            nc.tensor.matmul(actp[:, S:2 * S], wk[:], cT[:, s, :], start=True, stop=True)
            nc.tensor.matmul(dvep[:, 0:S], wq[:], xT[:, s, :], start=True, stop=True)
            nc.tensor.matmul(dvep[:, S:2 * S], cT[:, s, :], wv[:], start=True, stop=True).then_inc(qkv_done, 1)

        def max_scores(b, s, k):
            if k == 0:
                pe.wait_ge(qz_ready, b + 1)
                pe.wait_ge(kT_ready, b + 1)
            wait(pe, mx_ready, 4 * b + k - 1)
            for j in range(Q4):
                last = nc.tensor.matmul(maxp[k % 2][:, j * S:(j + 1) * S], lead(qz[:, s, Q4 * k + j, :]),
                                        lead(kT[:, s, :]), start=True, stop=True)
            last.then_inc(max_done, 1)

        def scores(b, s, k):
            pe.wait_ge(mx_ready, 4 * b + k + 1)
            wait(pe, exp_ready, 4 * b + k - 1)
            nc.tensor.matmul(tp[k % 2], kT[:, s, :], qz[:, s, Q4 * k:Q4 * k + Q4, :].rearrange("p h q -> p (h q)"),
                             start=True, stop=False)
            for j in range(Q4):
                h = Q4 * k + j
                last = nc.tensor.matmul(tp[k % 2][:, j * S:(j + 1) * S], mx[:, s, h:h + 1].to_broadcast([P, P]),
                                        negI[:], start=False, stop=(j == Q4 - 1))
            last.then_inc(t_done, 1)

        def values(b, s, k):
            pe.wait_ge(exp_ready, 4 * b + k + 1)
            if k == 0:
                pe.wait_ge(v_ready, b + 1)
                wait(pe, oev_ready, b)
            for j in range(Q4):
                last = nc.tensor.matmul(pv[32 * j:32 * j + 32, k * S:(k + 1) * S], v[:, s, Q4 * k + j, :],
                                        pT[:, k % 2, j * S:(j + 1) * S], start=True, stop=True)
            last.then_inc(pv_done, 1)

        def back_transposes(b, s):
            pe.wait_ge(oev_ready, b + 1)
            wait(pe, x1_ready, b)
            for i in range(Q4):
                last = nc.tensor.transpose(outp[:, i * S:(i + 1) * S], oev[:, s, i * S:(i + 1) * S], ident[:])
            last.then_inc(tr_done, 1)

        def o_transpose(b, s):
            pe.wait_ge(on_ready, b + 1)
            nc.tensor.transpose(outp[:, 0:S], on[:], ident[:]).then_inc(ot_done, 1)

        def output(b, s):
            pe.wait_ge(oT_ready, b + 1)
            nc.tensor.matmul(outp[:, S:2 * S], oT[:], wo[:], start=True, stop=True).then_inc(wo_done, 1)

        x_transpose(0, 0)
        projections(0, 0)
        max_scores(0, 0, 0)
        max_scores(0, 0, 1)

        def step(b, s):
            first, final = known(b, 0), known(b, B - 1)
            if not final:
                x_transpose(b + 1, 1 - s)
            for k in range(4):
                scores(b, s, k)
                if k < 2:
                    max_scores(b, s, k + 2)
                elif not final:
                    max_scores(b + 1, 1 - s, k - 2)
                if k == 0 and not first:
                    back_transposes(b - 1, 1 - s)
                if k == 0 and not final:
                    projections(b + 1, 1 - s)
                if k >= 1:
                    values(b, s, k - 1)
                if not first:
                    if k == 1:
                        o_transpose(b - 1, 1 - s)
                    if k == 2:
                        output(b - 1, 1 - s)
            values(b, s, 3)

        over_pairs(pe, B, step)
        back_transposes(B - 1, 1)
        o_transpose(B - 1, 1)
        output(B - 1, 1)

    def scalar_part(act):
        act.wait_ge(w_in, N_W)

        def x_copy(b, s):
            act.wait_ge(xt_done, b + 1)
            wait(act, qkv_done, b - 1)
            nc.scalar.copy(xT[:, s, :], actp[:, 0:S]).then_inc(xT_ready, 1)

        def k_copy(b, s):
            act.wait_ge(qkv_done, b + 1)
            wait(act, t_done, 4 * (b - 1))
            nc.scalar.activation(kT[:, s, :], actp[:, S:2 * S], ACT.Identity, bias=bk[:], scale=1.0).then_inc(kT_ready, 1)

        def exps(b, s, k):
            act.wait_ge(t_done, 4 * b + k + 1)
            wait(act, pv_done, 4 * b + k - 1)
            nc.scalar.activation(pT[:, k % 2, :], tp[k % 2], ACT.Exp, scale=SCALE).then_inc(exp_ready, 1)

        def pv_copy(b, s):
            act.wait_ge(pv_done, 4 * b + 4)
            wait(act, tr_done, b - 1)
            nc.scalar.copy(oev[:, s, :], pv).then_inc(oev_ready, 1)

        def o_copy(b, s):
            act.wait_ge(ot_done, b + 1)
            wait(act, wo_done, b)
            nc.scalar.copy(oT[:], outp[:, 0:S]).then_inc(oT_ready, 1)

        def mv_copy(b, s):
            wait_apart(act, consts, (ag2_done, b + 1))
            nc.scalar.copy(at(mv_out, b), ag2[:, s, :]).then_inc(mv2_done, 1)

        x_copy(0, 0)
        k_copy(0, 0)

        def step(b, s):
            first, final = known(b, 0), known(b, B - 1)
            if not (first or known(b, 1)):
                mv_copy(b - 2, s)
            if not first:
                pv_copy(b - 1, 1 - s)
            if not final:
                x_copy(b + 1, 1 - s)
            exps(b, s, 0)
            if not final:
                k_copy(b + 1, 1 - s)
            exps(b, s, 1)
            if not first:
                o_copy(b - 1, 1 - s)
            exps(b, s, 2)
            exps(b, s, 3)

        over_pairs(act, B, step)
        pv_copy(B - 1, 1)
        o_copy(B - 1, 1)
        mv_copy(B - 2, 0)
        mv_copy(B - 1, 1)

    def vector_part(dve):
        dve.wait_ge(cst, consts["n_ready"])
        dve.wait_ge(w_in, N_W)
        dve.wait_ge(ones_set, 1)

        def x_stats(b, s):
            loaded(dve, b, s)
            nc.vector.bn_stats(bn[:, s, :], at(x_res, b)).then_inc(bn_done, 1)
            wait_apart(dve, consts, (bn_done, b + 1), (rs_done, b - 1))
            nc.vector.bn_aggr(mv[:, s, :], bn[:, s, :]).then_inc(mv_done, 1)

        def x_norm(b, s):
            dve.wait_ge(mv_done, b + 1)
            dve.wait_ge(rs_done, b + 1)
            wait(dve, xt_done, b - 1)
            nc.vector.tensor_scalar(xn[:, s, :], at(x_res, b), mv[:, s, 0:1], rs[:, s, 1:2],
                                    ALU.subtract, ALU.mult).then_inc(xn_ready, 1)

        def q_spread(b, s):
            dve.wait_ge(qkv_done, b + 1)
            wait(dve, t_done, 4 * (b - 1))
            nc.vector.scalar_tensor_tensor(
                out=qz[:, s, :, :], in0=dvep[:, 0:S].unsqueeze(1).broadcast_to([P, H, S]), scalar=bq[:],
                in1=mask[:].unsqueeze(2).broadcast_to([P, H, S]), op0=ALU.add, op1=ALU.mult).then_inc(qz_ready, 1)

        def v_copy(b, s):
            wait(dve, pv_done, 4 * (b - 1))
            nc.vector.tensor_tensor(v[:, s, :, 0:HD], dvep[:, S:2 * S].rearrange("p (h d) -> p h d", h=H),
                                    bv_row[:].rearrange("p (h d) -> p h d", h=H), ALU.add).then_inc(v_ready, 1)

        def maxima(b, s, k):
            dve.wait_ge(max_done, 4 * b + k + 1)
            if k == 0:
                wait(dve, t_done, 4 * (b - 1))
            nc.vector.tensor_reduce(mx[:, s, Q4 * k:Q4 * k + Q4], maxp[k % 2].rearrange("p (h t) -> p h t", h=Q4),
                                    AX_X, ALU.max).then_inc(mx_ready, 1)

        def normalise(b, s):
            dve.wait_ge(tr_done, b + 1)
            o3 = outp.rearrange("p (h c) -> p h c", h=H)
            nc.vector.reciprocal(rden[:], o3[:, :, HD]).then_inc(rden_ready, 1)
            dve.wait_ge(rden_ready, b + 1)
            wait(dve, ot_done, b)
            nc.vector.tensor_tensor(on[:].rearrange("p (h d) -> p h d", h=H), o3[:, :, 0:HD],
                                    rden[:].unsqueeze(2).broadcast_to([P, H, HD]), ALU.mult).then_inc(on_ready, 1)

        def residual(b, s):
            dve.wait_ge(wo_done, b + 1)
            dve.wait_ge(xb_ready, b + 1)
            nc.vector.tensor_tensor(at(x_res, b), outp[:, S:2 * S], xb[:, s, :], ALU.add).then_inc(x1_ready, 1)
            wait_apart(dve, consts, (x1_ready, b + 1))
            nc.vector.bn_stats(bn2[:, s, :], at(x_res, b)).then_inc(bn2_done, 1)
            wait_apart(dve, consts, (bn2_done, b + 1), (mv2_done, b - 1))
            nc.vector.bn_aggr(ag2[:, s, :], bn2[:, s, :]).then_inc(ag2_done, 1)

        x_stats(0, 0)
        x_norm(0, 0)
        x_stats(1, 1)
        q_spread(0, 0)
        v_copy(0, 0)
        maxima(0, 0, 0)
        maxima(0, 0, 1)
        x_norm(1, 1)

        def step(b, s):
            first, late, final = known(b, 0), known(b, B - 2) or known(b, B - 1), known(b, B - 1)
            for k in range(4):
                if k < 2:
                    maxima(b, s, k + 2)
                elif not final:
                    maxima(b + 1, 1 - s, k - 2)
                if k == 0 and not first:
                    normalise(b - 1, 1 - s)
                if k == 0 and not final:
                    q_spread(b + 1, 1 - s)
                    v_copy(b + 1, 1 - s)
                if k == 1 and not late:
                    x_stats(b + 2, s)
                if k == 2:
                    if not late:
                        x_norm(b + 2, s)
                    if not first:
                        residual(b - 1, 1 - s)

        over_pairs(dve, B, step)
        normalise(B - 1, 1)
        residual(B - 1, 1)

    return dict(sync=sync_part, gpsimd=pool_part, tensor=tensor_part, scalar=scalar_part, vector=vector_part,
                done=(mv2_done, B))


def make_consts(nc, ctx):
    def sb(name, shape, dt=F32):
        return ctx.enter_context(nc.sbuf_tensor(name, shape, dt))

    ready = ctx.enter_context(nc.semaphore("consts_ready"))
    c = dict(ready=ready, ident=sb("ident", [P, P]), negI=sb("negI", [P, P], BF16), identb=sb("identb", [P, P], BF16),
             mask=sb("head_rows", [P, 16]), minus_half=sb("minus_half", [P, 32]), half=sb("half", [P, 32]))

    def pool_part(g):
        nc.gpsimd.memset(c["ident"][:], 0.0)
        nc.gpsimd.memset(c["negI"][:], 0.0)
        nc.gpsimd.memset(c["identb"][:], 0.0)
        nc.gpsimd.memset(c["minus_half"][:], -0.5)
        nc.gpsimd.memset(c["half"][:], 0.5)
        nc.gpsimd.memset(c["mask"][:], 1.0).then_inc(ready, 1)
        g.wait_ge(ready, 1)
        for name, fill in (("ident", 1.0), ("negI", -1.0), ("identb", 1.0)):
            nc.gpsimd.affine_select(out=c[name][:], in_=c[name][:], compare_op=ALU.not_equal, fill=fill, base=0,
                                    pattern=[[-1, P]], channel_multiplier=1).then_inc(ready, 1)
        nc.gpsimd.affine_select(out=c["mask"][:], in_=c["mask"][:], compare_op=ALU.is_ge, fill=0.0, base=0,
                                pattern=[[-8, 16]], channel_multiplier=1).then_inc(ready, 1)
        g.wait_ge(ready, 5)
        nc.gpsimd.affine_select(out=c["mask"][:], in_=c["mask"][:], compare_op=ALU.is_ge, fill=0.0, base=7,
                                pattern=[[8, 16]], channel_multiplier=-1).then_inc(ready, 1)

    c["n_ready"] = 6
    c["pool_part"] = pool_part
    return c


class Chain:

    def __init__(self, eng, sem):
        self.eng, self.sem, self.n = eng, sem, 0

    def then(self, ins):
        self.n += 1
        ins.then_inc(self.sem, 1)
        self.eng.wait_ge(self.sem, self.n)


def group(t, g):
    if isinstance(g, int):
        return t[:, g, :, :]
    return t[:, bass.ds(g, 1), :, :].rearrange("p a b d -> p (a b) d")


def expert_block(nc, ctx, space, consts, w, x_res, mv_in, psum, dram, before, xn2, pos_g):
    B, D = 32, P
    E, F = 8, 512
    FC = F // P
    G = 4
    NG = B // G
    CAP_S, CAP_MIN = 256, 4
    NT = B + E
    ZERO_ROW = NT * P

    def sb(name, shape, dt=F32):
        return space.enter_context(nc.sbuf_tensor("e_" + name, shape, dt))

    def sem(name):
        return ctx.enter_context(nc.semaphore(name))

    ident, half, minus_half, cst = consts["ident"], consts["half"], consts["minus_half"], consts["ready"]
    W1, W2 = sb("w1", [P, E, F]), sb("w2", [P, E * FC, D])
    b1_row, b1_col = sb("b1_row", [P, E, F]), sb("b1_col", [P, E * FC])
    gb1 = sb("gb1", [P, E * FC])
    b2_row = sb("b2_row", [P, E, D])
    Dc = sb("Dc", [P, E, D])
    Cc = sb("Cc", [P, D])
    waffT, wsq, wn = sb("waffT", [P, E]), sb("wsq", [P, E]), sb("wn", [P, E])
    thr = sb("thr", [P, 1])
    ones = sb("ones_f", [P, P])
    before_t = sb("before_t", [P, P], BF16)
    before_q = sb("before_q", [P, G, P])
    ones_b = sb("ones_b", [P, P], BF16)
    rs2, vpe = sb("rs2", [P, B]), sb("vpe", [P, B])
    xnorm = sb("xnorm", [P, B])
    xg = sb("xg", [P, 2, G * D])
    xgT = sb("xgT", [P, 2, G * D])
    num = sb("num", [P, NG, G * E])
    aff, den = sb("aff", [P, B, E]), sb("aff_den", [P, B, E])
    mval, tmp, score, smax = sb("mval", [P, B]), sb("r_tmp", [P, B, E]), sb("score", [P, B, E]), sb("smax", [P, B])
    tcr = sb("tcr", [P, B, E])
    weight = sb("weight", [P, E])
    red = sb("red", [P, 8])
    capi = sb("capi", [P, 2], I32)
    rT = sb("rT", [P, 4, P])
    aslot, tslot = sb("aslot", [E, 2, G, P]), sb("tslot", [E, 2, G, P])
    dd, ee = sb("dd", [P, G, P]), sb("ee", [P, G, P])
    cnt = sb("cnt", [P, NG, G])
    keep = sb("keep", [P, B])
    disp, dispb = sb("disp", [P, B, E]), sb("dispb", [P, B, E], BF16)
    cum = [sb(f"cum{i}", [P, B, E]) for i in range(2)]
    tot = sb("tot", [P, B, E])
    ne, nt = sb("ne", [P, E]), sb("ntl", [P, E])
    nti = sb("nti", [P, E], I32)
    inc = [sb(f"inc{i}", [P, E]) for i in range(2)]
    basee = sb("basee", [P, E])
    pos, act_ = sb("posf", [P, B]), sb("active", [P, B])
    trash = sb("trash", [P, B])
    pos_s = sb("pos_s", [P, B], I32)
    tile_no = sb("tile_no", [1, NT])
    cmp = sb("cmp", [1, NT, E])
    eidf, eid = sb("eidf", [1, NT]), sb("eid", [1, NT], I32)
    zeros = sb("zeros", [P, D])
    xt, xtT = sb("xt", [P, 2, D]), sb("xtT", [P, 2, D])
    hb, hT = sb("hb", [P, 2, F]), sb("hT", [P, 2, F])
    yt = sb("yt", [P, 2, D])

    w_in, p_set, z_out = sem("e_w_in"), sem("e_p_set"), sem("e_z_out")
    pool_seq, dve_seq = sem("e_pool_seq"), sem("e_dve_seq")
    xg_done, xn2_done = sem("e_xg_done"), sem("e_xn2_done")
    tp_done, xgT_done, num_done, numc_done = sem("e_tp_done"), sem("e_xgT_done"), sem("e_num_done"), sem("e_numc_done")
    rt_out = sem("e_rt_out")
    pe_route, dve_route, act_route, pool_route = sem("e_pe_route"), sem("e_dve_route"), sem("e_act_route"), sem("e_pool_route")
    wsum_done, d_done, sum_done, rt_done, pre_done = ((pe_route, k + 1) for k in range(5))
    wsumc_done, affs_done, tcr_done, z_done, disp_done, pos_done, dc_done = ((dve_route, k + 1) for k in range(7))
    wsq_done, gb1_done, ez_done, rtc_done = ((act_route, k + 1) for k in range(4))
    rs_done, den_done = ((pool_route, k + 1) for k in range(2))
    slot_in = [sem(f"e_slot_in{s}") for s in range(2)]
    a_done, cnt_done = sem("e_a_done"), sem("e_cnt")
    scat = sem("e_scat")
    xt_in = [sem(f"e_xt_in{s}") for s in range(2)]
    xtt_done, xtT_done, h_done, hb_done = sem("e_xtt"), sem("e_xtT"), sem("e_h"), sem("e_hb")
    ht_done, hT_done, y_done, yt_done = sem("e_ht"), sem("e_hT"), sem("e_y"), sem("e_yt")
    y_out = [sem(f"e_y_out{s}") for s in range(2)]
    N_W = 8 * 16

    xn_groups = xn2[:].rearrange("p (g b) d -> p g b d", b=G)

    def spread(t, n):
        return t.unsqueeze(2).broadcast_to([P, t.shape[1], n])

    def sync_weights(sp):
        sp.dma_start(W1[:], w["W1"].rearrange("e d f -> d e f")).then_inc(w_in, 16)
        sp.dma_start(W2[:], w["W2"].rearrange("e (c f) d -> f (e c) d", f=P)).then_inc(w_in, 16)
        sp.dma_start(b1_row[:], w["b1"].partition_broadcast(P)).then_inc(w_in, 16)
        sp.dma_start(b1_col[:], w["b1T"]).then_inc(w_in, 16)
        sp.dma_start(b2_row[:], w["b2"].partition_broadcast(P)).then_inc(w_in, 16)
        sp.dma_start(waffT[:], w["waffT"]).then_inc(w_in, 16)
        sp.dma_start(thr[:], w["thr"].partition_broadcast(P)).then_inc(w_in, 16)
        sp.dma_start(tile_no[:], w["tile_no"]).then_inc(w_in, 16)
        sp.wait_ge(p_set, 6)
        xs_tiles = dram["xs"].rearrange("(n p) d -> n p d", p=P)
        with sp.Fori(0, NT) as i:
            sp.dma_start(row(xs_tiles, i), zeros[:]).then_inc(z_out, 16)
        sp.dma_start(dram["ys"][ZERO_ROW:ZERO_ROW + P, :], zeros[:]).then_inc(z_out, 16)

    def sync_part(sp):
        sp.wait_ge(*rtc_done)
        sp.dma_start(dram["aT"].rearrange("(n q) t -> q n t", n=4), rT[:]).then_inc(rt_out, 16)
        sp.wait_ge(rt_out, 16)
        aT = dram["aT"].rearrange("(k b e) t -> k b e t", k=2, e=E)

        def slots(g, s):
            wait(sp, a_done, g - 1)
            for k, t in ((0, aslot), (1, tslot)):
                src = aT[k][G * g:G * g + G] if isinstance(g, int) else aT[k][bass.ds(G * g, G)]
                sp.dma_start(t[:, s, :, :], src.rearrange("b e t -> e b t")).then_inc(slot_in[s], 16)

        over_pairs(sp, NG, slots)
        sp.wait_ge(scat, 16 * B)
        xs_tiles = dram["xs"].rearrange("(n p) d -> n p d", p=P)

        def load(i, s):
            wait(sp, xtt_done, i - 1)
            sp.dma_start(xt[:, s, :], row(xs_tiles, i)).then_inc(xt_in[s], 16)

        load(0, 0)
        load(1, 1)
        over_pairs(sp, NT - 2, lambda i, s: load(i + 2, s))

    def pool_setup(g):
        nc.gpsimd.memset(ones[:], 1.0).then_inc(p_set, 1)
        nc.gpsimd.memset(ones_b[:], 1.0).then_inc(p_set, 1)
        nc.gpsimd.memset(before_t[:], 1.0).then_inc(p_set, 1)
        nc.gpsimd.memset(before_q[:], 1.0).then_inc(p_set, 1)
        nc.gpsimd.memset(zeros[:], 0.0).then_inc(p_set, 1)
        for e in range(E):
            last = nc.gpsimd.memset(weight[:, e:e + 1], float(E - e))
        last.then_inc(p_set, 1)
        g.wait_ge(p_set, 6)
        nc.gpsimd.affine_select(out=before_t[:], in_=before_t[:], compare_op=ALU.is_ge, fill=0.0, base=-1,
                                pattern=[[1, P]], channel_multiplier=-1).then_inc(p_set, 1)
        nc.gpsimd.affine_select(out=before_q[:], in_=before_q[:], compare_op=ALU.is_ge, fill=0.0, base=-1,
                                pattern=[[0, G], [-1, P]], channel_multiplier=1).then_inc(p_set, 1)
        nc.gpsimd.iota(trash[:], pattern=[[P, B]], base=NT * P, channel_multiplier=1,
                       allow_small_or_imprecise_dtypes=True).then_inc(p_set, 1)

    def pool_part(g):
        seq = Chain(g, pool_seq)
        g.wait_ge(before[0], before[1])
        seq.then(nc.gpsimd.tensor_scalar_add(vpe[:], mv_in[:, :, 1], EPS_BLOCK))
        nc.gpsimd.tensor_tensor(rs2[:], vpe[:], minus_half[:], ALU.pow).then_inc(pool_route, 1)
        g.wait_ge(*rs_done)
        seq.then(nc.gpsimd.tensor_scalar(vpe[:], mv_in[:, :, 1], float(D), None, ALU.mult))
        seq.then(nc.gpsimd.tensor_tensor(vpe[:], vpe[:], half[:], ALU.pow))
        seq.then(nc.gpsimd.tensor_tensor(xnorm[:], vpe[:], rs2[:], ALU.mult))
        g.wait_ge(*wsumc_done)
        seq.then(nc.gpsimd.tensor_tensor(wn[:], wsq[:], half[:, 0:E], ALU.pow))
        seq.then(nc.gpsimd.tensor_tensor(den[:], spread(xnorm[:], E), wn[:].unsqueeze(1).broadcast_to([P, B, E]), ALU.mult))
        nc.gpsimd.tensor_scalar_add(den[:], den[:], 1e-9).then_inc(pool_route, 1)
        g.wait_ge(*pos_done)
        g.wait_ge(xn2_done, NG)
        g.wait_ge(z_out, 16 * (NT + 1))
        for b in range(B):
            nc.gpsimd.indirect_dma_start(
                out=dram["xs"], out_offset=bass.IndirectOffsetOnAxis(ap=pos_s[:, b:b + 1].bitcast(U32), axis=0),
                in_=xn2[:, b, :], in_offset=None).then_inc(scat, 16)

    def tensor_part(pe, while_scattering):
        pe.wait_ge(w_in, N_W)
        pe.wait_ge(p_set, 9)
        pe.wait_ge(*wsq_done)
        pe.wait_ge(before[0], before[1])
        nc.tensor.matmul(psum[:, 7, 0:E], ones[:], wsq[:], start=True, stop=True).then_inc(pe_route, 1)

        def transposes(g, s):
            pe.wait_ge(xg_done, g + 1)
            wait(pe, xgT_done, g - 1)
            for j in range(G):
                last = nc.tensor.transpose(psum[:, s, j * P:(j + 1) * P], xg[:, s, j * P:(j + 1) * P], ident[:])
            last.then_inc(tp_done, 1)

        def affinities(g, s):
            pe.wait_ge(xgT_done, g + 1)
            wait(pe, numc_done, g - 1)
            for j in range(G):
                last = nc.tensor.matmul(psum[:, 2 + s, j * E:(j + 1) * E], xgT[:, s, j * P:(j + 1) * P], waffT[:],
                                        start=True, stop=True)
            last.then_inc(num_done, 1)

        transposes(0, 0)

        def step(g, s):
            if not known(g, NG - 1):
                transposes(g + 1, 1 - s)
            affinities(g, s)

        over_pairs(pe, NG, step)
        pe.wait_ge(*gb1_done)
        for e in range(E):
            for c in range(FC):
                last = nc.tensor.matmul(psum[:, 4 + e // 4, (e % 4) * P:(e % 4 + 1) * P],
                                        gb1[:, e * FC + c:e * FC + c + 1].to_broadcast([P, P]), W2[:, e * FC + c, :],
                                        start=(c == 0), stop=(c == FC - 1))
        last.then_inc(pe_route, 1)
        pe.wait_ge(*affs_done)
        nc.tensor.matmul(psum[:, 6, 0:1], ones[:], red[:, 0:1], start=True, stop=True).then_inc(pe_route, 1)
        pe.wait_ge(*tcr_done)
        for i, t in enumerate((aff, tcr)):
            for k in range(2):
                last = nc.tensor.transpose(psum[:, 0, (2 * i + k) * P:(2 * i + k + 1) * P],
                                           t[:].rearrange("p b e -> p (b e)")[:, k * P:(k + 1) * P], ident[:])
        last.then_inc(pe_route, 1)

        def own_affinity(g, s):
            if isinstance(g, int):
                pe.wait_ge(slot_in[s], 32 * (g // 2 + 1))
            else:
                pe.wait_ge(slot_in[s], (g - s) * 16 + 32)
            wait(pe, cnt_done, g - 1)
            for j in range(G):
                last = nc.tensor.matmul(psum[:, 1 + s, j * P:(j + 1) * P], tslot[:, s, j, :], aslot[:, s, j, :],
                                        start=True, stop=True)
            last.then_inc(a_done, 1)

        over_pairs(pe, NG, own_affinity)
        pe.wait_ge(*disp_done)
        flat = dispb[:].rearrange("p b e -> p (b e)")
        nc.tensor.matmul(psum[:, 3, 0:B * E], before_t[:], flat, start=True, stop=True)
        nc.tensor.matmul(psum[:, 3, B * E:2 * B * E], ones_b[:], flat, start=True, stop=True).then_inc(pe_route, 1)

        def x_transpose(i, s):
            pe.wait_ge(xt_in[s], 16 * (i // 2 + 1) if isinstance(i, int) else (i - s) * 8 + 16)
            wait(pe, xtT_done, i)
            nc.tensor.transpose(psum[:, 0, 0:P], xt[:, s, :], ident[:]).then_inc(xtt_done, 1)

        def up(i, s):
            e = pe.value_load(eid[0:1, bass.ds(i, 1)], min_val=0, max_val=E - 1)
            pe.wait_ge(xtT_done, i + 1)
            wait(pe, hb_done, i - 1)
            nc.tensor.matmul(psum[:, 1 + s, :], xtT[:, s, :], at(W1, e), start=True, stop=True).then_inc(h_done, 1)
            return e

        def h_transposes(i, s):
            pe.wait_ge(hb_done, i + 1)
            wait(pe, hT_done, i - 1)
            for c in range(FC):
                last = nc.tensor.transpose(psum[:, 3 + s, c * P:(c + 1) * P], hb[:, s, c * P:(c + 1) * P], ident[:])
            last.then_inc(ht_done, 1)

        def down(i, s):
            e = pe.value_load(eid[0:1, bass.ds(i, 1)], min_val=0, max_val=E - 1)
            pe.wait_ge(hT_done, i + 1)
            wait(pe, yt_done, i - 1)
            for c in range(FC):
                last = nc.tensor.matmul(psum[:, 5 + s, 0:D], hT[:, s, c * P:(c + 1) * P],
                                        W2[:, bass.ds(e * FC + c, 1), :].rearrange("p a d -> p (a d)"),
                                        start=(c == 0), stop=(c == FC - 1))
            last.then_inc(y_done, 1)

        pe.wait_ge(*pos_done)
        pe.wait_ge(*dc_done)
        while_scattering(pe)
        x_transpose(0, 0)
        up(0, 0)
        x_transpose(1, 1)

        def step(i, s):
            last_two = known(i, NT - 2) or known(i, NT - 1)
            h_transposes(i, s)
            if not known(i, NT - 1):
                up(i + 1, 1 - s)
            if not last_two:
                x_transpose(i + 2, s)
            down(i, s)

        over_pairs(pe, NT, step)

    def scalar_part(act):
        act.wait_ge(w_in, N_W)
        nc.scalar.activation(wsq[:], waffT[:], ACT.Square).then_inc(act_route, 1)

        def x_copies(g, s):
            act.wait_ge(xg_done, g + 1)
            nc.scalar.copy(group(xn_groups, g), xg[:, s, :].rearrange("p (b d) -> p b d", b=G)).then_inc(xn2_done, 1)
            act.wait_ge(tp_done, g + 1)
            wait(act, num_done, g - 1)
            nc.scalar.copy(xgT[:, s, :], psum[:, s, :]).then_inc(xgT_done, 1)

        over_pairs(act, NG, x_copies)
        nc.scalar.activation(gb1[:], b1_col[:], ACT.Gelu).then_inc(act_route, 1)
        act.wait_ge(*z_done)
        nc.scalar.activation(red[:, 2:3], red[:, 1:2], ACT.Exp, scale=-1.0).then_inc(act_route, 1)
        act.wait_ge(*rt_done)
        nc.scalar.copy(rT[:].rearrange("p n t -> p (n t)"), psum[:, 0, :]).then_inc(act_route, 1)

        def x_copy(i, s):
            act.wait_ge(xtt_done, i + 1)
            wait(act, h_done, i - 1)
            nc.scalar.copy(xtT[:, s, :], psum[:, 0, 0:P]).then_inc(xtT_done, 1)

        def gelu(i, s):
            act.wait_ge(ht_done, i + 1)
            wait(act, y_done, i - 1)
            nc.scalar.activation(hT[:, s, :], psum[:, 3 + s, :], ACT.Gelu).then_inc(hT_done, 1)

        ys_tiles = dram["ys"].rearrange("(n p) d -> n p d", p=P)

        def store(i, s):
            act.wait_ge(yt_done, i + 1)
            act.dma_start(row(ys_tiles, i), yt[:, s, :]).then_inc(y_out[s], 16)

        x_copy(0, 0)
        x_copy(1, 1)

        def step(i, s):
            gelu(i, s)
            if not known(i, 0):
                store(i - 1, 1 - s)
            if not (known(i, NT - 2) or known(i, NT - 1)):
                x_copy(i + 2, s)

        over_pairs(act, NT, step)
        store(NT - 1, 1)

    def vector_part(dve, while_scattering):
        seq = Chain(dve, dve_seq)
        dve.wait_ge(w_in, N_W)
        dve.wait_ge(p_set, 9)
        dve.wait_ge(before[0], before[1])
        dve.wait_ge(*wsum_done)
        nc.vector.tensor_copy(wsq[:], psum[:, 7, 0:E]).then_inc(dve_route, 1)
        dve.wait_ge(*rs_done)

        def x_norm(g, s):
            wait(dve, tp_done, g - 1)
            wait(dve, xn2_done, g - 1)
            for j in range(G):
                b = G * g + j
                mean = mv_in[:, b, 0:1] if isinstance(b, int) else mv_in[:, bass.ds(b, 1), 0:1].rearrange("p a c -> p (a c)")
                rs = rs2[:, b:b + 1] if isinstance(b, int) else rs2[:, bass.ds(b, 1)]
                last = nc.vector.tensor_scalar(xg[:, s, j * D:(j + 1) * D], at(x_res, b), mean, rs, ALU.subtract, ALU.mult)
            last.then_inc(xg_done, 1)

        def num_copy(g, s):
            dve.wait_ge(num_done, g + 1)
            nc.vector.tensor_copy(at(num, g), psum[:, 2 + s, 0:G * E]).then_inc(numc_done, 1)

        x_norm(0, 0)
        x_norm(1, 1)

        def step(g, s):
            num_copy(g, s)
            if not (known(g, NG - 2) or known(g, NG - 1)):
                x_norm(g + 2, s)

        over_pairs(dve, NG, step)
        dve.wait_ge(*den_done)
        seq.then(nc.vector.reciprocal(den[:], den[:]))
        dve.wait_ge(numc_done, NG)
        seq.then(nc.vector.tensor_tensor(aff[:], num[:].rearrange("p g (b e) -> p (g b) e", e=E), den[:], ALU.mult))
        nc.vector.tensor_reduce(red[:, 0:1], aff[:].rearrange("p b e -> p (b e)"), AX_X, ALU.add).then_inc(dve_route, 1)
        seq.then(nc.vector.tensor_reduce(mval[:], aff[:], AX_X, ALU.max))
        seq.then(nc.vector.tensor_tensor(tmp[:], aff[:], spread(mval[:], E), ALU.is_equal))
        seq.then(nc.vector.tensor_tensor(score[:], tmp[:], weight[:].unsqueeze(1).broadcast_to([P, B, E]), ALU.mult))
        seq.then(nc.vector.tensor_reduce(smax[:], score[:], AX_X, ALU.max))
        nc.vector.tensor_tensor(tcr[:], score[:], spread(smax[:], E), ALU.is_equal).then_inc(dve_route, 1)
        dve.wait_ge(*sum_done)
        nc.vector.scalar_tensor_tensor(out=red[:, 1:2], in0=psum[:, 6, 0:1], scalar=1.0 / (B * P * E), in1=thr[:],
                                       op0=ALU.mult, op1=ALU.subtract).then_inc(dve_route, 1)
        dve.wait_ge(*ez_done)
        seq.then(nc.vector.tensor_scalar_add(red[:, 3:4], red[:, 2:3], 1.0))
        seq.then(nc.vector.reciprocal(red[:, 4:5], red[:, 3:4]))
        seq.then(nc.vector.tensor_scalar(red[:, 5:6], red[:, 4:5], float(CAP_S), None, ALU.mult))

        def floor(dst, src, whole, high):
            seq.then(nc.vector.tensor_copy(whole, src))
            seq.then(nc.vector.tensor_copy(dst, whole))
            seq.then(nc.vector.tensor_tensor(high, dst, src, ALU.is_gt))
            seq.then(nc.vector.tensor_tensor(dst, dst, high, ALU.subtract))

        floor(red[:, 6:7], red[:, 5:6], capi[:, 0:1], red[:, 7:8])
        seq.then(nc.vector.tensor_scalar(red[:, 6:7], red[:, 6:7], float(CAP_MIN), float(CAP_S), ALU.max, ALU.min))

        def count_before(g, s):
            n = 3 * g
            dve.wait_ge(a_done, g + 1)
            if isinstance(g, int):
                m = mval[:, G * g:G * g + G]
            else:
                m = mval[:, bass.ds(G * g, G)]
            nc.vector.tensor_tensor(dd[:], psum[:, 1 + s, :].rearrange("p (b t) -> p b t", b=G),
                                    m.unsqueeze(2).broadcast_to([P, G, P]), ALU.subtract).then_inc(cnt_seq, 1)
            dve.wait_ge(cnt_seq, n + 1)
            nc.vector.scalar_tensor_tensor(out=ee[:], in0=dd[:], scalar=0.0, in1=before_q[:], op0=ALU.is_equal,
                                           op1=ALU.mult).then_inc(cnt_seq, 1)
            dve.wait_ge(cnt_seq, n + 2)
            nc.vector.scalar_tensor_tensor(out=ee[:], in0=dd[:], scalar=0.0, in1=ee[:], op0=ALU.is_gt,
                                           op1=ALU.add).then_inc(cnt_seq, 1)
            dve.wait_ge(cnt_seq, n + 3)
            nc.vector.tensor_reduce(at(cnt, g), ee[:], AX_X, ALU.add).then_inc(cnt_done, 1)

        over_pairs(dve, NG, count_before)
        dve.wait_ge(cnt_done, NG)
        seq.then(nc.vector.tensor_scalar(keep[:], cnt[:].rearrange("p g b -> p (g b)"), red[:, 6:7], None, ALU.is_lt))
        seq.then(nc.vector.tensor_tensor(disp[:], tcr[:], spread(keep[:], E), ALU.mult))
        nc.vector.tensor_copy(dispb[:], disp[:]).then_inc(dve_route, 1)
        dve.wait_ge(*pre_done)
        flat = "p b e -> p (b e)"
        seq.then(nc.vector.tensor_copy(tot[:].rearrange(flat), psum[:, 3, B * E:2 * B * E]))
        seq.then(nc.vector.tensor_copy(cum[0][:], tot[:]))
        k, src, dst = 1, 0, 1
        while k < B:
            seq.then(nc.vector.tensor_copy(cum[dst][:, 0:k, :], cum[src][:, 0:k, :]))
            seq.then(nc.vector.tensor_tensor(cum[dst][:, k:B, :], cum[src][:, k:B, :], cum[src][:, 0:B - k, :], ALU.add))
            k, src, dst = 2 * k, dst, src
        seq.then(nc.vector.tensor_scalar(ne[:], cum[src][:, B - 1, :], float(P - 1), 1.0 / P, ALU.add, ALU.mult))
        seq.then(nc.vector.tensor_tensor(cum[src][:], cum[src][:], tot[:], ALU.subtract))
        floor(nt[:], ne[:], nti[:], basee[:])
        seq.then(nc.vector.tensor_copy(inc[0][:], nt[:]))
        k, a, z = 1, 0, 1
        while k < E:
            seq.then(nc.vector.tensor_copy(inc[z][:, 0:k], inc[a][:, 0:k]))
            seq.then(nc.vector.tensor_tensor(inc[z][:, k:E], inc[a][:, k:E], inc[a][:, 0:E - k], ALU.add))
            k, a, z = 2 * k, z, a
        seq.then(nc.vector.tensor_tensor(basee[:], inc[a][:], nt[:], ALU.subtract))
        seq.then(nc.vector.tensor_scalar(basee[:], basee[:], float(P), None, ALU.mult))
        seq.then(nc.vector.tensor_tensor(tmp[:].rearrange(flat), psum[:, 3, 0:B * E], cum[src][:].rearrange(flat), ALU.add))
        seq.then(nc.vector.tensor_tensor(tmp[:], tmp[:], basee[:].unsqueeze(1).broadcast_to([P, B, E]), ALU.add))
        seq.then(nc.vector.tensor_tensor(tmp[:], tmp[:], disp[:], ALU.mult))
        seq.then(nc.vector.tensor_reduce(pos[:], tmp[:], AX_X, ALU.add))
        seq.then(nc.vector.tensor_reduce(act_[:], disp[:], AX_X, ALU.add))
        seq.then(nc.vector.tensor_scalar(act_[:], act_[:], -1.0, 1.0, ALU.mult, ALU.add))
        seq.then(nc.vector.tensor_tensor(trash[:], trash[:], act_[:], ALU.mult))
        seq.then(nc.vector.tensor_tensor(trash[:], trash[:], pos[:], ALU.add))
        seq.then(nc.vector.tensor_copy(pos_s[:], trash[:]))
        seq.then(nc.vector.scalar_tensor_tensor(out=pos[:], in0=act_[:], scalar=float(ZERO_ROW), in1=pos[:],
                                                op0=ALU.mult, op1=ALU.add))
        seq.then(nc.vector.tensor_copy(pos_g[:], pos[:]))
        seq.then(nc.vector.tensor_tensor(cmp[:], inc[a][0:1, :].unsqueeze(1).broadcast_to([1, NT, E]),
                                         tile_no[:].unsqueeze(2).broadcast_to([1, NT, E]), ALU.is_le))
        seq.then(nc.vector.tensor_reduce(eidf[:], cmp[:], AX_X, ALU.add))
        seq.then(nc.vector.tensor_scalar(eidf[:], eidf[:], float(E - 1), None, ALU.min))
        nc.vector.tensor_copy(eid[:], eidf[:]).then_inc(dve_route, 1)
        dve.wait_ge(*d_done)
        for k in range(2):
            last = nc.vector.tensor_copy(Dc[:, 4 * k:4 * k + 4, :].rearrange("p e d -> p (e d)"), psum[:, 4 + k, :])
        last.then_inc(dve_route, 1)
        dve.wait_ge(*dc_done)
        seq.then(nc.vector.tensor_tensor(b2_row[:], b2_row[:], Dc[:], ALU.add))
        seq.then(nc.vector.tensor_reduce(Cc[:], b2_row[:].rearrange("p e d -> p d e"), AX_X, ALU.add))
        seq.then(nc.vector.tensor_tensor(x_res[:], x_res[:], Cc[:].unsqueeze(1).broadcast_to([P, B, D]), ALU.add))
        while_scattering(dve)
        dve.wait_ge(*pos_done)

        def h_bias(i, s):
            e = dve.value_load(eid[0:1, bass.ds(i, 1)], min_val=0, max_val=E - 1)
            dve.wait_ge(h_done, i + 1)
            wait(dve, ht_done, i - 1)
            nc.vector.tensor_tensor(hb[:, s, :], psum[:, 1 + s, :], at(b1_row, e), ALU.add).then_inc(hb_done, 1)

        def y_out_copy(i, s):
            e = dve.value_load(eid[0:1, bass.ds(i, 1)], min_val=0, max_val=E - 1)
            dve.wait_ge(y_done, i + 1)
            if not (known(i, 0) or known(i, 1)):
                dve.wait_ge(y_out[s], 16 * (i // 2) if isinstance(i, int) else (i - s) * 8)
            nc.vector.tensor_tensor(yt[:, s, :], psum[:, 5 + s, 0:D], at(Dc, e), ALU.subtract).then_inc(yt_done, 1)

        h_bias(0, 0)

        def tile(i, s):
            if not known(i, NT - 1):
                h_bias(i + 1, 1 - s)
            y_out_copy(i, s)

        over_pairs(dve, NT, tile)

    cnt_seq = sem("e_cnt_seq")
    return dict(sync_weights=sync_weights, sync=sync_part, pool_setup=pool_setup, gpsimd=pool_part, tensor=tensor_part,
                scalar=scalar_part, vector=vector_part, y_out=y_out, y_total=16 * NT // 2,
                yt_done=(yt_done, NT))


def cross_attention_block(nc, ctx, consts, w, x_res, mv_out, psum, before, gathered):
    B, S, D = 32, P, P
    H, HD = 16, 64
    NP = H // 2
    Q4 = 4
    SCALE = float(H) ** -0.5
    BIG = 3.0e38

    def sb(name, shape, dt=F32):
        return ctx.enter_context(nc.sbuf_tensor("a_" + name, shape, dt))

    def sem(name):
        return ctx.enter_context(nc.semaphore("a_" + name))

    negI, ident, minus_half = consts["negI"], consts["ident"], consts["minus_half"]
    WqT, WkT = sb("WqT", [P, NP, D]), sb("WkT", [P, NP, D])
    A = sb("A", [P, H, D])
    Wv, Wo = sb("Wv", [P, H * HD]), sb("Wo", [P, NP, D])
    nk = sb("nk", [P, 2])
    Wn1, Wn = sb("Wn1", [P, H]), sb("Wn", [P, P])
    s1, b1, sc_, bc = sb("s1", [P, 1]), sb("b1", [P, 1]), sb("sc", [P, 1]), sb("bc", [P, 1])
    so_row, bo_row = sb("so_row", [P, D]), sb("bo_row", [P, D])
    nv_row = sb("nv_row", [P, HD])
    nv_res = sb("nv_res", [P, HD])
    nvh = [sb(f"nv{i}", [P, HD], BF16) for i in range(3)]
    nvsel = sb("nvsel", [P, HD])
    parts = sb("parts", [P, 4])
    sel = sb("sel", [P, H])
    NV, ON = sb("NV", [P, H, HD], BF16), sb("ON", [P, H, HD], BF16)
    eps2 = sb("eps2", [P, 2])
    onescol = sb("onescol", [P, HD])
    ones_row = sb("ones_row", [1, P], BF16)
    mask8, mask_bias = sb("mask8", [P, B], mybir.dt.uint8), sb("mask_bias", [P, B])
    mrow8, mask_row = sb("mrow8", [1, B, S], mybir.dt.uint8), sb("mask_row", [1, B, S], BF16)
    cin = sb("cin", [P, 2, D])
    bn = sb("bn", [P, 2, 2, 6])
    mv = sb("mv", [P, 2, 2, 2])
    rs, rt = sb("rs", [P, 2, 2]), sb("rt", [P, 2, 2])
    xn, cn = sb("xn", [P, 2, D]), sb("cn", [P, 2, D])
    xT, cT = sb("xT", [P, 2, S]), sb("cT", [P, 2, S])
    G = sb("G", [P, 2, H, S])
    v = sb("v", [P, 2, H * HD])
    sn = sb("sn", [P, 2, H])
    mxf, mx = sb("mxf", [P, 2, Q4]), sb("mx", [P, 2, H], BF16)
    mx_rep = sb("mx_rep", [P, P], BF16)
    pT = sb("pT", [P, 2, Q4 * S])
    pn, pnr, pnb = sb("pn", [P, S]), sb("pnr", [P, S]), sb("pnb", [P, S], BF16)
    rd = sb("rd", [P, 512])
    oT = sb("oT", [P, 2, NP * S])
    o = sb("o", [P, D])
    bno, mvo, rso = sb("bno", [P, 6]), sb("mvo", [P, 2]), sb("rso", [P, 2])
    on, on2 = sb("on", [P, D]), sb("on2", [P, D])
    xb = sb("xb", [P, D])
    bn3, ag3 = sb("bn3", [P, 6]), sb("ag3", [P, 2, 2])
    oev, dev = sb("oev", [P, 2, 512]), sb("dev", [P, 2, 512])

    w_in, p_set, dve_seq, setup_done = sem("w_in"), sem("p_set"), sem("dve_seq"), sem("setup_done")
    sa_done, sac_done = sem("sa_done"), sem("sac_done")
    cin_ld = [sem(f"cin_ld{s}") for s in range(2)]
    x2_ready, bnx_done, mvx_done = sem("x2_ready"), sem("bnx_done"), sem("mvx_done")
    pool_rs, rs_ready, xcn_ready = sem("pool_rs"), sem("rs_ready"), sem("xcn_ready")
    xt_done, xcT_ready = sem("xt_done"), sem("xcT_ready")
    g_done, ga_ready, g1_ready, g3_ready = sem("g_done"), sem("ga_ready"), sem("g1_ready"), sem("g3_ready")
    va_done, vv_done, va_ready, vv_ready = sem("va_done"), sem("vv_done"), sem("va_ready"), sem("vv_ready")
    sn_done, sn_ready = sem("sn_done"), sem("sn_ready")
    max_done, mxf_ready, mx_ready, rep_ready = sem("max_done"), sem("mxf_ready"), sem("mx_ready"), sem("rep_ready")
    t_done, exp_ready, pv_done = sem("t_done"), sem("exp_ready"), sem("pv_done")
    ns_done, pn_ready, split_seq, pnb_ready, null_done = sem("ns_done"), sem("pn_ready"), sem("split_seq"), sem("pnb_ready"), sem("null_done")
    rd_ready, oT_ready, out_done, o_ready = sem("rd_ready"), sem("oT_ready"), sem("out_done"), sem("o_ready")
    bno_done, mvo_done, rso_t, rso_ready = sem("bno_done"), sem("mvo_done"), sem("rso_t"), sem("rso_ready")
    ag3_done, ev_ready = sem("ag3_done"), sem("ev_ready")
    xb_ready, on_done, on2_done, x3_ready, bn3_done, mv3_done = (sem("xb_ready"), sem("on_done"), sem("on2_done"),
                                                                sem("x3_ready"), sem("bn3_done"), sem("mv3_done"))
    N_W = 18 * 16
    maxp = [psum[:, i, :] for i in (0, 1)]
    tp = [psum[:, i, :] for i in (2, 3)]
    op, dp = psum[:, 4, :], psum[:, 5, :]
    ap, vp = psum[:, 6, :], psum[:, 7, :]

    y, y_in, pos_g, gather_src = gathered["y"], gathered["sems"], gathered["pos_g"], gathered["src"]

    def slot_wait(eng, sems, b, s):
        eng.wait_ge(sems[s], 16 * (b // 2 + 1) if isinstance(b, int) else (b - s) * 8 + 16)

    def sync_weights(sp):
        for t, n in ((WqT, "WqT"), (WkT, "WkT"), (Wo, "Wo")):
            sp.dma_start(t[:], w[n].rearrange("(n p) d -> p n d", p=P)).then_inc(w_in, 16)
        sp.dma_start(Wv[:], w["Wkv"][:, H * HD:]).then_inc(w_in, 16)
        for t, n in ((s1, "ln1_s"), (b1, "ln1_b"), (sc_, "lnc_s"), (bc, "lnc_b")):
            sp.dma_start(t[:], w[n].rearrange("(d a) -> d a", a=1)).then_inc(w_in, 16)
        sp.dma_start(so_row[:], w["lno_s"].partition_broadcast(P)).then_inc(w_in, 16)
        sp.dma_start(bo_row[:], w["lno_b"].partition_broadcast(P)).then_inc(w_in, 16)
        sp.dma_start(nv_row[:], w["null_kv"][1].partition_broadcast(P)).then_inc(w_in, 16)
        sp.wait_ge(p_set, 1)
        for j in range(2):
            sp.dma_start(nk[j * HD:(j + 1) * HD, j:j + 1], w["null_kv"][0].rearrange("(d a) -> d a", a=1)).then_inc(w_in, 16)
        sp.dma_start(mask8[:], w["maskT"]).then_inc(w_in, 16)
        sp.dma_start(mrow8[:], w["mask"].rearrange("(a b) s -> a b s", a=1)).then_inc(w_in, 16)
        sp.dma_start(parts[:], w["parts"]).then_inc(w_in, 16)
        sp.dma_start(sel[:], w["sel"]).then_inc(w_in, 16)
        sp.dma_start(eps2[:], w["eps2"]).then_inc(w_in, 16)

    def sync_part(sp):
        def step(b, s):
            wait(sp, xcn_ready, b - 1)
            sp.dma_start(cin[:, s, :], row(w["ctx"], b)).then_inc(cin_ld[s], 16)

        over_pairs(sp, B, step)

    def pool_setup(g):
        nc.gpsimd.memset(nk[:], 0.0).then_inc(p_set, 1)
        nc.gpsimd.memset(onescol[:], 1.0).then_inc(p_set, 1)
        nc.gpsimd.memset(ones_row[:], 1.0).then_inc(p_set, 1)

    def pool_part(g):
        def gather(b):
            if b >= 2:
                g.wait_ge(y_in[b % 2], 16 * (b // 2))
            nc.gpsimd.indirect_dma_start(
                out=y[:, b, :], out_offset=None, in_=gather_src,
                in_offset=bass.IndirectOffsetOnAxis(ap=pos_g[:, b:b + 1].bitcast(U32), axis=0)).then_inc(y_in[b % 2], 16)

        def rsqrt(b, s):
            n = 6 * b
            g.wait_ge(mvx_done, 2 * b + 2)
            wait(g, xcn_ready, b - 1)
            nc.gpsimd.tensor_tensor(rt[:, s, :], mv[:, s, :, 1], eps2[:], ALU.add).then_inc(pool_rs, 1)
            g.wait_ge(pool_rs, n + 1)
            nc.gpsimd.tensor_tensor(rs[:, s, :], rt[:, s, :], minus_half[:, 0:2], ALU.pow).then_inc(pool_rs, 1)
            g.wait_ge(pool_rs, n + 2)
            nc.gpsimd.tensor_tensor(rt[:, s, 0:1], mv[:, s, 0, 1:2], rs[:, s, 0:1], ALU.mult).then_inc(pool_rs, 1)
            g.wait_ge(pool_rs, n + 3)
            nc.gpsimd.tensor_tensor(rt[:, s, 1:2], rt[:, s, 0:1], rs[:, s, 0:1], ALU.mult).then_inc(pool_rs, 1)
            g.wait_ge(pool_rs, n + 4)
            nc.gpsimd.tensor_scalar_add(rt[:, s, 0:1], rt[:, s, 1:2], EPS_L1).then_inc(pool_rs, 1)
            g.wait_ge(pool_rs, n + 5)
            nc.gpsimd.tensor_tensor(rt[:, s, 1:2], rt[:, s, 0:1], minus_half[:, 0:1], ALU.pow).then_inc(pool_rs, 1)
            g.wait_ge(pool_rs, n + 6)
            nc.gpsimd.tensor_tensor(rs[:, s, 0:1], rs[:, s, 0:1], rt[:, s, 1:2], ALU.mult).then_inc(rs_ready, 1)

        def out_rsqrt(b, s):
            g.wait_ge(mvo_done, b + 1)
            wait(g, on_done, b)
            nc.gpsimd.tensor_scalar_add(rso[:, 0:1], mvo[:, 1:2], EPS_L1).then_inc(rso_t, 1)
            g.wait_ge(rso_t, b + 1)
            nc.gpsimd.tensor_tensor(rso[:, 1:2], rso[:, 0:1], minus_half[:, 0:1], ALU.pow).then_inc(rso_ready, 1)

        def x_plus(b, s):
            g.wait_ge(x2_ready, b + 1)
            wait(g, x3_ready, b)
            nc.gpsimd.tensor_tensor(xb[:], x_res[:, b, :], bo_row[:], ALU.add).then_inc(xb_ready, 1)

        def mv_copy(b, s):
            g.wait_ge(ag3_done, b + 1)
            nc.gpsimd.tensor_copy(mv_out[:, b, :], ag3[:, s, :]).then_inc(mv3_done, 1)

        for q in gathered["ready"]:
            g.wait_ge(*q)
        gather(0)
        gather(1)
        rsqrt(0, 0)
        gather(2)
        rsqrt(1, 1)
        gather(3)
        for b in range(B):
            s = b % 2
            if b + 4 < B:
                gather(b + 4)
            if b + 2 < B:
                rsqrt(b + 2, s)
            if b >= 2:
                mv_copy(b - 2, s)
            if b >= 1:
                out_rsqrt(b - 1, 1 - s)
                x_plus(b - 1, 1 - s)
        mv_copy(B - 2, 0)
        out_rsqrt(B - 1, 1)
        x_plus(B - 1, 1)
        mv_copy(B - 1, 1)

    def tensor_setup(pe):
        pe.wait_ge(w_in, N_W)
        pe.wait_ge(p_set, 3)
        for h in range(H):
            r = (h % 2) * HD
            last = nc.tensor.matmul(psum[:, 2 * (h % 2) + h // 8, (h // 2 % 4) * P:(h // 2 % 4 + 1) * P], WqT[r:r + HD, h // 2, :],
                                    WkT[r:r + HD, h // 2, :], start=True, stop=True)
        for p in range(NP):
            last = nc.tensor.matmul(psum[:, 4, 2 * p:2 * p + 2], WqT[:, p, :], nk[:], start=True, stop=True)
        last.then_inc(sa_done, 1)
        pe.wait_ge(setup_done, 1)

    def tensor_part(pe):
        for q in before:
            pe.wait_ge(*q)

        def transposes(b, s):
            pe.wait_ge(xcn_ready, b + 1)
            wait(pe, va_ready, b)
            nc.tensor.transpose(ap[:, 0:S], xn[:, s, :], ident[:])
            nc.tensor.transpose(ap[:, S:2 * S], cn[:, s, :], ident[:]).then_inc(xt_done, 1)

        def projection(b, s, k):
            pe.wait_ge(xcT_ready, b + 1)
            if k == 1:
                wait(pe, sn_ready, b)
            if k == 2:
                pe.wait_ge(ga_ready, 2 * b + 1)
            if k == 3:
                wait(pe, o_ready, b - 1)
                pe.wait_ge(g1_ready, b + 1)
            bank = (ap, vp)[k % 2]
            for j in range(Q4):
                last = nc.tensor.matmul(bank[:, j * S:(j + 1) * S], A[:, Q4 * k + j, :], xT[:, s, :], start=True, stop=True)
            last.then_inc(g_done, 1)

        def values_a(b, s):
            wait(pe, pn_ready, b)
            pe.wait_ge(ga_ready, 2 * b + 2)
            nc.tensor.matmul(ap, cT[:, s, :], Wv[:, 0:512], start=True, stop=True).then_inc(va_done, 1)

        def values_v(b, s):
            pe.wait_ge(g3_ready, b + 1)
            nc.tensor.matmul(vp, cT[:, s, :], Wv[:, 512:1024], start=True, stop=True).then_inc(vv_done, 1)

        def null_scores(b, s):
            pe.wait_ge(vv_ready, b + 1)
            nc.tensor.matmul(vp[:, 0:H], lead(xT[:, s, :]), lead(Wn1[:, :]), start=True, stop=True).then_inc(sn_done, 1)

        def max_scores(b, s, k):
            quarter = ((ga_ready, 2 * b + 1), (g1_ready, b + 1), (ga_ready, 2 * b + 2), (g3_ready, b + 1))[k]
            wait_apart(pe, consts, quarter, (mxf_ready, 4 * b + k - 1))
            m = at(mask_row[0:1], b)
            nc.tensor.matmul(maxp[k % 2].rearrange("p (h t) -> p h t", h=Q4), ones_row[:],
                             m.unsqueeze(1).broadcast_to([1, Q4, S]), start=True, stop=False)
            for j in range(Q4):
                last = nc.tensor.matmul(maxp[k % 2][:, j * S:(j + 1) * S], lead(G[:, s, Q4 * k + j, :]),
                                        lead(cT[:, s, :]), start=False, stop=(j == Q4 - 1))
            last.then_inc(max_done, 1)

        def scores(b, s, k):
            pe.wait_ge(mx_ready, 4 * b + k + 1)
            wait(pe, exp_ready, 4 * b + k - 1)
            nc.tensor.matmul(tp[k % 2], cT[:, s, :], G[:, s, Q4 * k:Q4 * k + Q4, :].rearrange("p h q -> p (h q)"),
                             start=True, stop=False)
            for j in range(Q4):
                h = Q4 * k + j
                last = nc.tensor.matmul(tp[k % 2][:, j * S:(j + 1) * S], mx[:, s, h:h + 1].to_broadcast([P, P]),
                                        negI[:], start=False, stop=(j == Q4 - 1))
            last.then_inc(t_done, 1)

        def null_weights(b, s):
            pe.wait_ge(rep_ready, b + 1)
            if known(b, B - 1):
                pe.wait_ge(va_ready, B)
            else:
                pe.wait_ge(ga_ready, 2 * b + 4)
            nc.tensor.matmul(ap[:, 0:S], Wn[:], xT[:, s, :], start=True, stop=False)
            nc.tensor.matmul(ap[:, 0:S], mx_rep[:], negI[:], start=False, stop=True).then_inc(ns_done, 1)

        def weighted(b, s, k):
            pe.wait_ge(exp_ready, 4 * b + k + 1)
            if k == 0:
                pe.wait_ge(va_ready, b + 1)
                wait(pe, ev_ready, 2 * b)
            if k == 2:
                pe.wait_ge(vv_ready, b + 1)
                pe.wait_ge(ev_ready, 2 * b + 1)
            for j in range(Q4):
                h, r = Q4 * k + j, (j % 2) * HD
                c = ((h // 2) % 4) * S
                nc.tensor.matmul(op[r:r + HD, c:c + S], v[:, s, h * HD:(h + 1) * HD], pT[:, k % 2, j * S:(j + 1) * S],
                                 start=(k % 2 == 0 and j < 2), stop=False, skip_group_check=True)
            p2 = pT[:, k % 2, :].rearrange("p (a e q) -> p e a q", a=2, e=2)
            for e in range(2):
                r, c = e * HD, (k % 2) * 2 * S
                last = nc.tensor.matmul(dp[r:r + HD, c:c + 2 * S].rearrange("p (a q) -> p a q", a=2), onescol[:], p2[:, e, :, :],
                                        start=(k % 2 == 0), stop=False, skip_group_check=True)
            last.then_inc(pv_done, 1)

        def null_part(b, s, half):
            pe.wait_ge(pnb_ready, b + 1)
            for i in range(4):
                p = 4 * half + i
                nc.tensor.matmul(op[:, i * S:(i + 1) * S], NV[:, 2 * p:2 * p + 2, :].rearrange("p h d -> p (h d)"), pnb[:],
                                 start=False, stop=True, skip_group_check=True)
                last = nc.tensor.matmul(dp[:, i * S:(i + 1) * S], ON[:, 2 * p:2 * p + 2, :].rearrange("p h d -> p (h d)"),
                                        pnb[:], start=False, stop=True, skip_group_check=True)
            last.then_inc(null_done, 1)

        transposes(0, 0)
        for k in range(4):
            projection(0, 0, k)
        values_a(0, 0)
        values_v(0, 0)
        null_scores(0, 0)
        max_scores(0, 0, 0)
        max_scores(0, 0, 1)

        def step(b, s):
            first, final = known(b, 0), known(b, B - 1)
            if not final:
                transposes(b + 1, 1 - s)
            scores(b, s, 0)
            max_scores(b, s, 2)
            if not final:
                projection(b + 1, 1 - s, 0)
                projection(b + 1, 1 - s, 1)
            scores(b, s, 1)
            max_scores(b, s, 3)
            weighted(b, s, 0)
            if not first:
                if final:
                    pe.wait_ge(sn_ready, B)
                output_(b - 1, 1 - s, final)
            if not final:
                projection(b + 1, 1 - s, 2)
            scores(b, s, 2)
            null_weights(b, s)
            if not final:
                projection(b + 1, 1 - s, 3)
                max_scores(b + 1, 1 - s, 0)
            weighted(b, s, 1)
            null_part(b, s, 0)
            if not final:
                values_v(b + 1, 1 - s)
            scores(b, s, 3)
            if not final:
                max_scores(b + 1, 1 - s, 1)
                null_scores(b + 1, 1 - s)
                values_a(b + 1, 1 - s)
            weighted(b, s, 2)
            weighted(b, s, 3)
            null_part(b, s, 1)

        def output_(b, s, final):
            pe.wait_ge(oT_ready, 2 * b + 2)
            if not final:
                pe.wait_ge(g1_ready, b + 3)
            for p in range(NP):
                last = nc.tensor.matmul(vp[:, 0:D], oT[:, s, p * S:(p + 1) * S], Wo[:, p, :], start=(p == 0), stop=(p == NP - 1))
            last.then_inc(out_done, 1)

        over_pairs(pe, B, step)
        pe.wait_ge(o_ready, B - 1)
        output_(B - 1, 1, True)

    def scalar_part(act):
        act.wait_ge(w_in, N_W)

        def xc_copy(b, s):
            act.wait_ge(xt_done, b + 1)
            wait(act, t_done, 4 * (b - 1))
            nc.scalar.activation(xT[:, s, :], ap[:, 0:S], ACT.Identity, bias=b1[:], scale=s1[:])
            nc.scalar.activation(cT[:, s, :], ap[:, S:2 * S], ACT.Identity, bias=bc[:], scale=sc_[:]).then_inc(xcT_ready, 1)

        def g_copy(b, s, k):
            act.wait_ge(g_done, 4 * b + k + 1)
            bank, ready = (vp, g1_ready) if k == 1 else (ap, ga_ready)
            nc.scalar.copy(G[:, s, Q4 * k:Q4 * k + Q4, :].rearrange("p h q -> p (h q)"), bank).then_inc(ready, 1)

        def v_copy(b, s):
            act.wait_ge(va_done, b + 1)
            wait(act, pv_done, 4 * (b - 1))
            nc.scalar.copy(v[:, s, 0:512], ap).then_inc(va_ready, 1)

        def exps(b, s, k):
            wait_apart(act, consts, (t_done, 4 * b + k + 1), (pv_done, 4 * b + k - 1))
            bias = mask_bias[:, b:b + 1] if isinstance(b, int) else mask_bias[:, bass.ds(b, 1)]
            nc.scalar.activation(pT[:, k % 2, :], tp[k % 2], ACT.Exp, scale=SCALE, bias=bias).then_inc(exp_ready, 1)

        def null_exp(b, s):
            act.wait_ge(ns_done, b + 1)
            wait(act, pnb_ready, b)
            nc.scalar.activation(pn[:], ap[:, 0:S], ACT.Exp, scale=SCALE).then_inc(pn_ready, 1)

        def ev_copy(b, s, half):
            act.wait_ge(null_done, 2 * b + half + 1)
            wait(act, oT_ready, 2 * b + half - 1)
            nc.scalar.copy(oev[:, half, :], op)
            nc.scalar.copy(dev[:, half, :], dp).then_inc(ev_ready, 1)

        act.wait_ge(setup_done, 1)
        xc_copy(0, 0)
        g_copy(0, 0, 0)
        g_copy(0, 0, 1)
        g_copy(0, 0, 2)
        v_copy(0, 0)

        def step(b, s):
            final = known(b, B - 1)
            if not known(b, 0):
                ev_copy(b - 1, 1 - s, 1)
            if not final:
                xc_copy(b + 1, 1 - s)
            exps(b, s, 0)
            if not final:
                g_copy(b + 1, 1 - s, 0)
                g_copy(b + 1, 1 - s, 1)
            exps(b, s, 1)
            if not final:
                g_copy(b + 1, 1 - s, 2)
            exps(b, s, 2)
            null_exp(b, s)
            ev_copy(b, s, 0)
            exps(b, s, 3)
            if not final:
                v_copy(b + 1, 1 - s)

        over_pairs(act, B, step)
        ev_copy(B - 1, 1, 1)

    def vector_setup(dve):
        seq = Chain(dve, dve_seq)
        dve.wait_ge(w_in, N_W)
        dve.wait_ge(p_set, 3)
        dve.wait_ge(sa_done, 1)
        for k in range(4):
            nc.vector.tensor_copy(A[:, 8 * (k % 2) + k // 2:8 * (k % 2) + 8:2, :], psum[:, k, :].rearrange("p (h d) -> p h d", h=4))
        seq.then(nc.vector.tensor_copy(Wn1[:], psum[:, 4, 0:H]))
        nc.vector.tensor_copy(Wn[:].rearrange("p (r h) -> p r h", r=8), Wn1[:].unsqueeze(1).broadcast_to([P, 8, H]))
        seq.then(nc.vector.tensor_copy(nvh[0][:], nv_row[:]))
        seq.then(nc.vector.tensor_tensor(nv_res[:], nv_row[:], nvh[0][:], ALU.subtract))
        seq.then(nc.vector.tensor_copy(nvh[1][:], nv_res[:]))
        seq.then(nc.vector.tensor_tensor(nv_res[:], nv_res[:], nvh[1][:], ALU.subtract))
        seq.then(nc.vector.tensor_copy(nvh[2][:], nv_res[:]))
        seq.then(nc.vector.tensor_scalar(nvsel[:], nvh[0][:], parts[:, 0:1], None, ALU.mult))
        for i in (1, 2):
            seq.then(nc.vector.scalar_tensor_tensor(out=nvsel[:], in0=nvh[i][:], scalar=parts[:, i:i + 1], in1=nvsel[:],
                                                    op0=ALU.mult, op1=ALU.add))
        heads = sel[:].unsqueeze(2).broadcast_to([P, H, HD])
        seq.then(nc.vector.tensor_tensor(NV[:], heads, nvsel[:].unsqueeze(1).broadcast_to([P, H, HD]), ALU.mult))
        seq.then(nc.vector.tensor_scalar(ON[:], heads, parts[:, 3:4], None, ALU.mult))
        seq.then(nc.vector.tensor_scalar(mask_bias[:], mask8[:], -1.0, BIG, ALU.add, ALU.mult))
        nc.vector.tensor_scalar(mask_row[:], mrow8[:], -1.0, BIG, ALU.add, ALU.mult).then_inc(setup_done, 1)

    def vector_part(dve):
        def stats(b, s):
            slot_wait(dve, y_in, b, s)
            nc.vector.tensor_tensor(at(x_res, b), at(x_res, b), at(y, b), ALU.add).then_inc(x2_ready, 1)
            slot_wait(dve, cin_ld, b, s)
            nc.vector.bn_stats(bn[:, s, 1, :], cin[:, s, :]).then_inc(bnx_done, 1)
            wait_apart(dve, consts, (x2_ready, b + 1))
            nc.vector.bn_stats(bn[:, s, 0, :], at(x_res, b)).then_inc(bnx_done, 1)
            wait_apart(dve, consts, (bnx_done, 2 * b + 2), (rs_ready, b - 1))
            nc.vector.bn_aggr(mv[:, s, 0, :], bn[:, s, 0, :]).then_inc(mvx_done, 1)
            nc.vector.bn_aggr(mv[:, s, 1, :], bn[:, s, 1, :]).then_inc(mvx_done, 1)

        def norm(b, s):
            dve.wait_ge(mvx_done, 2 * b + 2)
            dve.wait_ge(rs_ready, b + 1)
            wait(dve, xt_done, b - 1)
            nc.vector.tensor_scalar(xn[:, s, :], at(x_res, b), mv[:, s, 0, 0:1], rs[:, s, 0:1], ALU.subtract, ALU.mult)
            nc.vector.tensor_scalar(cn[:, s, :], cin[:, s, :], mv[:, s, 1, 0:1], rs[:, s, 1:2],
                                    ALU.subtract, ALU.mult).then_inc(xcn_ready, 1)

        def g_copy(b, s, k):
            dve.wait_ge(g_done, 4 * b + k + 1)
            wait(dve, t_done, 4 * (b - 1))
            nc.vector.tensor_copy(G[:, s, Q4 * k:Q4 * k + Q4, :].rearrange("p h q -> p (h q)"), vp).then_inc(g3_ready, 1)

        def v_copy(b, s):
            dve.wait_ge(vv_done, b + 1)
            wait(dve, pv_done, 4 * (b - 1))
            nc.vector.tensor_copy(v[:, s, 512:1024], vp).then_inc(vv_ready, 1)

        def null_copy(b, s):
            dve.wait_ge(sn_done, b + 1)
            nc.vector.tensor_copy(sn[:, s, :], vp[:, 0:H]).then_inc(sn_ready, 1)

        def maxima(b, s, k):
            dve.wait_ge(max_done, 4 * b + k + 1)
            if k == 0:
                wait(dve, t_done, 4 * (b - 1))
            nc.vector.tensor_reduce(mxf[:, k % 2, :], maxp[k % 2].rearrange("p (h t) -> p h t", h=Q4), AX_X, ALU.max).then_inc(mxf_ready, 1)

        def with_null(b, s, k):
            dve.wait_ge(mxf_ready, 4 * b + k + 1)
            dve.wait_ge(sn_ready, b + 1)
            nc.vector.tensor_tensor(mx[:, s, Q4 * k:Q4 * k + Q4], mxf[:, k % 2, :], sn[:, s, Q4 * k:Q4 * k + Q4], ALU.max).then_inc(mx_ready, 1)

        def replicate(b, s):
            dve.wait_ge(mx_ready, 4 * b + 4)
            wait(dve, ns_done, b)
            nc.vector.tensor_copy(mx_rep[:].rearrange("p (r h) -> p r h", r=8), mx[:, s, :].unsqueeze(1).broadcast_to([P, 8, H])).then_inc(rep_ready, 1)

        def split(b, s):
            n = 4 * b
            dve.wait_ge(pn_ready, b + 1)
            wait(dve, null_done, 2 * b)
            nc.vector.tensor_copy(pnb[:], pn[:]).then_inc(split_seq, 1)
            dve.wait_ge(split_seq, n + 1)
            nc.vector.tensor_tensor(pnr[64:128, :], pn[64:128, :], pnb[64:128, :], ALU.subtract).then_inc(split_seq, 1)
            dve.wait_ge(split_seq, n + 2)
            nc.vector.tensor_copy(pnb[64:128, :], pnr[64:128, :]).then_inc(split_seq, 1)
            dve.wait_ge(split_seq, n + 3)
            nc.vector.tensor_tensor(pnr[96:128, :], pnr[96:128, :], pnb[96:128, :], ALU.subtract).then_inc(split_seq, 1)
            dve.wait_ge(split_seq, n + 4)
            nc.vector.tensor_copy(pnb[96:128, :], pnr[96:128, :]).then_inc(pnb_ready, 1)

        def reciprocals(b, s, half, part):
            dve.wait_ge(ev_ready, 2 * b + half + 1)
            wait(dve, oT_ready, 2 * b + half)
            cols = slice(part * 256, part * 256 + 256)
            nc.vector.reciprocal(rd[:, cols], dev[:, half, cols]).then_inc(rd_ready, 1)

        def divide(b, s, half):
            dve.wait_ge(rd_ready, 4 * b + 2 * half + 2)
            if half == 0:
                wait(dve, out_done, b - 1)
            nc.vector.tensor_tensor(oT[:, s, half * 512:(half + 1) * 512], oev[:, half, :], rd[:], ALU.mult).then_inc(oT_ready, 1)

        def out_stats(b, s):
            dve.wait_ge(out_done, b + 1)
            nc.vector.tensor_copy(o[:], vp[:, 0:D]).then_inc(o_ready, 1)
            dve.wait_ge(o_ready, b + 1)
            nc.vector.bn_stats(bno[:], o[:]).then_inc(bno_done, 1)
            wait_apart(dve, consts, (bno_done, b + 1))
            nc.vector.bn_aggr(mvo[:], bno[:]).then_inc(mvo_done, 1)

        def out_norm(b, s):
            dve.wait_ge(rso_ready, b + 1)
            nc.vector.tensor_scalar(on[:], o[:], mvo[:, 0:1], rso[:, 1:2], ALU.subtract, ALU.mult).then_inc(on_done, 1)
            dve.wait_ge(on_done, b + 1)
            nc.vector.tensor_tensor(on2[:], on[:], so_row[:], ALU.mult).then_inc(on2_done, 1)
            dve.wait_ge(on2_done, b + 1)
            dve.wait_ge(xb_ready, b + 1)
            nc.vector.tensor_tensor(at(x_res, b), on2[:], xb[:], ALU.add).then_inc(x3_ready, 1)
            wait_apart(dve, consts, (x3_ready, b + 1))
            nc.vector.bn_stats(bn3[:], at(x_res, b)).then_inc(bn3_done, 1)
            wait_apart(dve, consts, (bn3_done, b + 1), (mv3_done, b - 1))
            nc.vector.bn_aggr(ag3[:, s, :], bn3[:]).then_inc(ag3_done, 1)

        stats(0, 0)
        norm(0, 0)
        stats(1, 1)
        g_copy(0, 0, 3)
        v_copy(0, 0)
        null_copy(0, 0)
        norm(1, 1)
        for k in range(2):
            maxima(0, 0, k)
        for k in range(2):
            with_null(0, 0, k)

        def step(b, s):
            first, final = known(b, 0), known(b, B - 1)
            late = final or known(b, B - 2)
            if not first:
                reciprocals(b - 1, 1 - s, 1, 0)
            maxima(b, s, 2)
            if not first:
                reciprocals(b - 1, 1 - s, 1, 1)
            with_null(b, s, 2)
            if not first:
                divide(b - 1, 1 - s, 1)
            maxima(b, s, 3)
            with_null(b, s, 3)
            replicate(b, s)
            if not late:
                stats(b + 2, s)
            if not first:
                out_stats(b - 1, 1 - s)
            if not late:
                norm(b + 2, s)
            split(b, s)
            if not final:
                g_copy(b + 1, 1 - s, 3)
                maxima(b + 1, 1 - s, 0)
            if not first:
                out_norm(b - 1, 1 - s)
            if not final:
                v_copy(b + 1, 1 - s)
                null_copy(b + 1, 1 - s)
                with_null(b + 1, 1 - s, 0)
            reciprocals(b, s, 0, 0)
            reciprocals(b, s, 0, 1)
            divide(b, s, 0)
            if not final:
                maxima(b + 1, 1 - s, 1)
                with_null(b + 1, 1 - s, 1)

        over_pairs(dve, B, step)
        reciprocals(B - 1, 1, 1, 0)
        reciprocals(B - 1, 1, 1, 1)
        divide(B - 1, 1, 1)
        out_stats(B - 1, 1)
        out_norm(B - 1, 1)

    return dict(sync_weights=sync_weights, sync=sync_part, pool_setup=pool_setup, gpsimd=pool_part, tensor=tensor_part,
                tensor_setup=tensor_setup, vector_setup=vector_setup,
                scalar=scalar_part, vector=vector_part, done=(mv3_done, B))


def bit_ffn_block(nc, ctx, consts, w, x_res, mv_in, psum, before, out):
    B, S, D, F = 32, P, P, 512
    FC = F // P
    M = 1.5 * 2.0 ** 23
    FLOOR = 1e-5

    def sb(name, shape, dt=F32):
        return ctx.enter_context(nc.sbuf_tensor("f_" + name, shape, dt))

    def sem(name):
        return ctx.enter_context(nc.semaphore("f_" + name))

    identb, minus_half = consts["identb"], consts["minus_half"]
    wf = sb("wf", [P, 3, F])
    wq = sb("wq", [P, 3, F], BF16)
    wt = sb("wt", [P, 3, F])
    wsum, wmean, wrec = sb("wsum", [P, 4]), sb("wmean", [P, 4]), sb("wrec", [P, 4])
    step_w = sb("step_w", [P, 4])
    ones = sb("ones", [P, P])
    big_m = sb("big_m", [P, 1])
    vpe, rs = sb("vpe", [P, B]), sb("rs", [P, B])
    xc, xn = sb("xc", [P, 2, D]), sb("xn", [P, 2, D])
    am, amc, rc, sc = sb("am", [P, 2]), sb("amc", [P, 2]), sb("rc", [P, 2]), sb("sc", [P, 2])
    sg_all, su_all = sb("sg_all", [P, B]), sb("su_all", [P, B])
    xt, xq, xqT = sb("xt", [P, 2, D]), sb("xq", [P, 2, D], BF16), sb("xqT", [P, 2 * S], BF16)
    gate, h = sb("gate", [P, 2, F]), sb("h", [P, 2, F])
    hm, hmc, hr, hs, hd = (sb(n, [P, 2]) for n in ("hm", "hmc", "hr", "hs", "hd"))
    ht = sb("ht", [P, 2, F])
    hq, hqT = sb("hq", [P, 2, F], BF16), sb("hqT", [P, 2, F], BF16)
    x4 = sb("x4", [P, 2, D])

    w_in, p_set, dve_seq, wsum_done, wsum_all, wq_done = (sem(n) for n in ("w_in", "p_set", "dve_seq", "wsum_done", "wsum_all", "wq_done"))
    vpe_done, rs_done, x_seq, xq_ready = sem("vpe_done"), sem("rs_done"), sem("x_seq"), sem("xq_ready")
    xt_done, xqT_ready, gu_done, gate_ready = sem("xt_done"), sem("xqT_ready"), sem("gu_done"), sem("gate_ready")
    h_ready, h_seq, hs_ready, ht_ready, hq_ready = sem("h_ready"), sem("h_seq"), sem("hs_ready"), sem("ht_ready"), sem("hq_ready")
    htr_done, hqT_ready, down_done, x4_ready = sem("htr_done"), sem("hqT_ready"), sem("down_done"), sem("x4_ready")
    stored = [sem(f"stored{s}") for s in range(2)]
    xtp, htp = psum[:, 0, :].bitcast(BF16)[:, 0:2 * S], psum[:, 5, :].bitcast(BF16)[:, 0:F]
    gp, up, dp = (1, 2), (3, 4), (6, 7)

    def cols(t, b, n=1):
        return t[:, b:b + n] if isinstance(b, int) else t[:, bass.ds(b, n)]

    def batches(t, b, n=2):
        return t[:, b:b + n, :] if isinstance(b, int) else t[:, bass.ds(b, n), :]

    def sync_weights(sp):
        sp.dma_start(wf[:, 0, :], w["gateT"]).then_inc(w_in, 16)
        sp.dma_start(wf[:, 1, :], w["upT"]).then_inc(w_in, 16)
        sp.dma_start(wf[:, 2, :].rearrange("p (c d) -> p c d", c=FC), w["downT"].rearrange("(c p) d -> p c d", p=P)).then_inc(w_in, 16)

    def sync_part(sp):
        def step(b, s):
            sp.wait_ge(x4_ready, b + 1)
            sp.dma_start(row(out, b), x4[:, s, :]).then_inc(stored[s], 16)

        over_pairs(sp, B, step)
        for s in range(2):
            sp.wait_ge(stored[s], 16 * (B // 2))

    def pool_setup(g):
        nc.gpsimd.memset(ones[:], 1.0).then_inc(p_set, 1)
        nc.gpsimd.memset(big_m[:], M).then_inc(p_set, 1)

    def pool_part(g):
        g.wait_ge(*before)
        nc.gpsimd.tensor_scalar_add(vpe[:], mv_in[:, :, 1], EPS_BLOCK).then_inc(vpe_done, 1)
        g.wait_ge(vpe_done, 1)
        nc.gpsimd.tensor_tensor(rs[:], vpe[:], minus_half[:], ALU.pow).then_inc(rs_done, 1)

    def tensor_part(pe):
        pe.wait_ge(p_set, 2)
        pe.wait_ge(*before)
        pe.wait_ge(wsum_done, 1)
        nc.tensor.matmul(psum[:, 6, 0:3], ones[:], wsum[:, 0:3], start=True, stop=True).then_inc(wsum_all, 1)
        pe.wait_ge(wq_done, 1)

        def x_transposes(b):
            pe.wait_ge(xq_ready, (b >> 1) + 1)
            wait(pe, xqT_ready, b >> 1)
            for j in range(2):
                last = nc.tensor.transpose(xtp[:, j * S:(j + 1) * S], xq[:, j, :], identb[:])
            last.then_inc(xt_done, 1)

        def gate_up(b, s):
            if s == 0:
                pe.wait_ge(xqT_ready, (b >> 1) + 1)
            wait(pe, gate_ready, b - 1)
            wait(pe, h_ready, b - 1)
            nc.tensor.matmul(psum[:, gp[s], :], xqT[:, s * S:(s + 1) * S], wq[:, 0, :], start=True, stop=True)
            nc.tensor.matmul(psum[:, up[s], :], xqT[:, s * S:(s + 1) * S], wq[:, 1, :], start=True, stop=True).then_inc(gu_done, 1)

        def h_transposes(b, s):
            pe.wait_ge(hq_ready, b + 1)
            wait(pe, hqT_ready, b)
            for c in range(FC):
                last = nc.tensor.transpose(htp[:, c * S:(c + 1) * S], hq[:, s, c * P:(c + 1) * P], identb[:])
            last.then_inc(htr_done, 1)

        def down(b, s):
            pe.wait_ge(hqT_ready, b + 1)
            wait(pe, x4_ready, b - 1)
            for c in range(FC):
                last = nc.tensor.matmul(psum[:, dp[s], 0:D], hqT[:, s, c * S:(c + 1) * S], wq[:, 2, c * D:(c + 1) * D],
                                        start=(c == 0), stop=(c == FC - 1))
            last.then_inc(down_done, 1)

        x_transposes(0)
        gate_up(0, 0)
        gate_up(1, 1)

        def step(b, s):
            late = known(b, B - 2) or known(b, B - 1)
            h_transposes(b, s)
            if s == 0 and not late:
                x_transposes(b + 2)
            if not known(b, 0):
                down(b - 1, 1 - s)
            if not late:
                gate_up(b + 2, s)

        over_pairs(pe, B, step)
        down(B - 1, 1)

    def scalar_part(act):
        def x_copy(b):
            act.wait_ge(xt_done, (b >> 1) + 1)
            wait(act, gu_done, b)
            nc.scalar.copy(xqT[:], xtp).then_inc(xqT_ready, 1)

        def silu(b, s):
            act.wait_ge(gu_done, b + 1)
            wait(act, h_ready, b - 1)
            nc.scalar.activation(gate[:, s, :], psum[:, gp[s], :], ACT.Silu, scale=cols(sg_all, b)).then_inc(gate_ready, 1)

        def h_scale(b, s):
            act.wait_ge(hs_ready, b + 1)
            wait(act, hq_ready, b - 1)
            nc.scalar.activation(ht[:, s, :], h[:, s, :], ACT.Identity, scale=hs[:, s:s + 1], bias=big_m[:]).then_inc(ht_ready, 1)

        def h_copy(b, s):
            act.wait_ge(htr_done, b + 1)
            wait(act, down_done, b - 1)
            nc.scalar.copy(hqT[:, s, :], htp).then_inc(hqT_ready, 1)

        act.wait_ge(p_set, 2)
        x_copy(0)
        silu(0, 0)
        h_scale(0, 0)

        def step(b, s):
            if not known(b, B - 1):
                silu(b + 1, 1 - s)
            h_copy(b, s)
            if s == 0 and not known(b, B - 2):
                x_copy(b + 2)
            if not known(b, B - 1):
                h_scale(b + 1, 1 - s)

        over_pairs(act, B, step)

    def vector_part(dve):
        seq = Chain(dve, dve_seq)
        dve.wait_ge(w_in, 3 * 16)
        for i in range(3):
            last = nc.vector.tensor_reduce(wsum[:, i:i + 1], wf[:, i, :], AX_X, ALU.add, apply_absolute_value=True)
        last.then_inc(wsum_done, 1)
        dve.wait_ge(wsum_all, 1)
        seq.then(nc.vector.tensor_scalar(wmean[:, 0:3], psum[:, 6, 0:3], 1.0 / (D * F), FLOOR, ALU.mult, ALU.max))
        seq.then(nc.vector.reciprocal(wrec[:, 0:3], wmean[:, 0:3]))
        nc.vector.tensor_scalar(step_w[:, 0:3], wmean[:, 0:3], 1.0 / 127.0, None, ALU.mult)
        for i in range(3):
            seq.then(nc.vector.tensor_scalar(wt[:, i, :], wf[:, i, :], wrec[:, i:i + 1], M, ALU.mult, ALU.add))
            seq.then(nc.vector.tensor_scalar(wt[:, i, :], wt[:, i, :], -M, -1.0, ALU.add, ALU.max))
            ins = nc.vector.tensor_scalar(wq[:, i, :], wt[:, i, :], 1.0, None, ALU.min)
        ins.then_inc(wq_done, 1)
        dve.wait_ge(rs_done, 1)

        def quantise_x(b):
            p = b >> 1
            n = 6 * p

            def then(i, ins):
                ins.then_inc(x_seq, 1)
                dve.wait_ge(x_seq, n + i)

            for j in range(2):
                c = b + j
                mean = mv_in[:, c, 0:1] if isinstance(c, int) else mv_in[:, bass.ds(c, 1), 0:1].rearrange("p a c -> p (a c)")
                last = nc.vector.tensor_scalar(xn[:, j, :], at(x_res, c), mean, cols(rs, c), ALU.subtract, ALU.mult)
            then(1, last)
            then(2, nc.vector.tensor_reduce(am[:], xn[:], AX_X, ALU.max, apply_absolute_value=True))
            then(3, nc.vector.tensor_scalar(amc[:], am[:], FLOOR, None, ALU.max))
            then(4, nc.vector.reciprocal(rc[:], amc[:]))
            nc.vector.tensor_scalar(cols(sg_all, b, 2), amc[:], step_w[:, 0:1], None, ALU.mult)
            nc.vector.tensor_scalar(cols(su_all, b, 2), amc[:], step_w[:, 1:2], None, ALU.mult)
            then(5, nc.vector.tensor_scalar(sc[:], rc[:], 127.0, None, ALU.mult))
            for j in range(2):
                last = nc.vector.tensor_scalar(xt[:, j, :], xn[:, j, :], sc[:, j:j + 1], M, ALU.mult, ALU.add)
            then(6, last)
            wait(dve, xt_done, p)
            nc.vector.tensor_scalar(xq[:], xt[:], -M, 127.0, ALU.add, ALU.min).then_inc(xq_ready, 1)

        def multiply(b, s):
            dve.wait_ge(gate_ready, b + 1)
            wait(dve, ht_ready, b - 1)
            nc.vector.scalar_tensor_tensor(out=h[:, s, :], in0=psum[:, up[s], :], scalar=cols(su_all, b), in1=gate[:, s, :],
                                           op0=ALU.mult, op1=ALU.mult).then_inc(h_ready, 1)

        def h_steps(b, s):
            n = 3 * b
            dve.wait_ge(h_ready, b + 1)
            nc.vector.tensor_reduce(hm[:, s:s + 1], h[:, s, :], AX_X, ALU.max, apply_absolute_value=True).then_inc(h_seq, 1)
            dve.wait_ge(h_seq, n + 1)
            nc.vector.tensor_scalar(hmc[:, s:s + 1], hm[:, s:s + 1], FLOOR, None, ALU.max).then_inc(h_seq, 1)
            dve.wait_ge(h_seq, n + 2)
            nc.vector.reciprocal(hr[:, s:s + 1], hmc[:, s:s + 1]).then_inc(h_seq, 1)
            nc.vector.tensor_scalar(hd[:, s:s + 1], hmc[:, s:s + 1], step_w[:, 2:3], None, ALU.mult)
            dve.wait_ge(h_seq, n + 3)
            wait(dve, ht_ready, b - 1)
            nc.vector.tensor_scalar(hs[:, s:s + 1], hr[:, s:s + 1], 127.0, None, ALU.mult).then_inc(hs_ready, 1)

        def h_round(b, s):
            dve.wait_ge(ht_ready, b + 1)
            wait(dve, htr_done, b - 1)
            nc.vector.tensor_scalar(hq[:, s, :], ht[:, s, :], -M, 127.0, ALU.add, ALU.min).then_inc(hq_ready, 1)

        def finish(b, s):
            dve.wait_ge(down_done, b + 1)
            if not (known(b, 0) or known(b, 1)):
                dve.wait_ge(stored[s], 16 * (b // 2) if isinstance(b, int) else (b - s) * 8)
            nc.vector.scalar_tensor_tensor(out=x4[:, s, :], in0=psum[:, dp[s], 0:D], scalar=hd[:, s:s + 1],
                                           in1=at(x_res, b), op0=ALU.mult, op1=ALU.add).then_inc(x4_ready, 1)

        quantise_x(0)
        quantise_x(2)
        multiply(0, 0)
        h_steps(0, 0)

        def step(b, s):
            h_round(b, s)
            if not known(b, B - 1):
                multiply(b + 1, 1 - s)
            if not known(b, 0):
                finish(b - 1, 1 - s)
            if not known(b, B - 1):
                h_steps(b + 1, 1 - s)
            if s == 0 and not (known(b, B - 4) or known(b, B - 2)):
                quantise_x(b + 4)

        over_pairs(dve, B, step, tail=4)
        finish(B - 1, 1)

    return dict(sync_weights=sync_weights, sync=sync_part, pool_setup=pool_setup, gpsimd=pool_part, tensor=tensor_part,
                scalar=scalar_part, vector=vector_part)


def two_layers(nc, d, out):
    B = 32
    E = 8
    n_tiles = B + E
    dram = dict(xs=nc.dram_tensor("sorted_x", ((n_tiles + B) * P, P), F32, kind="Internal").ap(),
                ys=nc.dram_tensor("sorted_y", ((n_tiles + 1) * P, P), F32, kind="Internal").ap(),
                aT=nc.dram_tensor("routing_T", (4 * P, P), F32, kind="Internal").ap())
    with ExitStack() as ctx:
        def sb(name, shape, dt=F32):
            return ctx.enter_context(nc.sbuf_tensor(name, shape, dt))

        x_res = sb("x_res", [P, B, P])
        mv1, mv3 = sb("mv1", [P, B, 2]), sb("mv3", [P, B, 2])
        xy = sb("xy", [P, B, P])
        pos_g = sb("pos_g", [P, B], I32)
        psum = ctx.enter_context(nc.psum_tensor("psum", [P, 8, 512], F32))
        y_in = [ctx.enter_context(nc.semaphore(f"y_in{s}")) for s in range(2)]
        consts = make_consts(nc, ctx)
        with ExitStack() as layer0:
            l0 = self_attention_block(nc, ctx, layer0, consts, d["x"], d["ctxT"],
                                      {n: d["L0_" + n] for n in ("Wq", "Wk", "Wv", "Wo", "bq", "bk", "bv", "bo")},
                                      x_res, mv1, psum)
            layer0.enter_context(nc.sbuf_tensor("layer1_constants_end", [P, 1664], F32))
            ex = expert_block(nc, ctx, layer0, consts,
                              {n: d["E_" + n] for n in ("W1", "W2", "b1", "b1T", "b2", "waffT", "thr", "tile_no")},
                              x_res, mv1, psum, dram, l0["done"], xy, pos_g)
        experts_done = [ex["yt_done"], (ex["y_out"][0], ex["y_total"]), (ex["y_out"][1], ex["y_total"])]
        at = cross_attention_block(nc, ctx, consts,
                                   {n[2:]: t for n, t in d.items() if n.startswith("A_")} | dict(ctx=d["ctx"]),
                                   x_res, mv3, psum, experts_done,
                                   dict(y=xy, sems=y_in, pos_g=pos_g, src=dram["ys"], ready=experts_done))
        ff = bit_ffn_block(nc, ctx, consts, {n: d["F_" + n] for n in ("gateT", "upT", "downT")},
                           x_res, mv3, psum, at["done"], out)
        block = ctx.enter_context(nc.Block())

        @block.sync
        def _(sp):
            l0["sync"](sp, lambda: ex["sync_weights"](sp))
            sp.wait_ge(*l0["done"])
            at["sync_weights"](sp)
            ex["sync"](sp)
            for q in experts_done:
                sp.wait_ge(*q)
            ff["sync_weights"](sp)
            at["sync"](sp)
            ff["sync"](sp)

        @block.gpsimd
        def _(g):
            consts["pool_part"](g)
            ex["pool_setup"](g)
            l0["gpsimd"](g)
            g.wait_ge(*l0["done"])
            at["pool_setup"](g)
            ex["gpsimd"](g)
            at["gpsimd"](g)
            ff["pool_setup"](g)
            ff["gpsimd"](g)

        @block.tensor
        def _(pe):
            l0["tensor"](pe)
            ex["tensor"](pe, at["tensor_setup"])
            at["tensor"](pe)
            ff["tensor"](pe)

        @block.scalar
        def _(act):
            l0["scalar"](act)
            ex["scalar"](act)
            at["scalar"](act)
            ff["scalar"](act)

        @block.vector
        def _(dve):
            l0["vector"](dve)
            ex["vector"](dve, at["vector_setup"])
            at["vector"](dve)
            ff["vector"](dve)


def kernel(x, ctx_1024, mask_BxS2_bf1, L0_xattn_Wq, L0_xattn_bq, L0_xattn_Wk, L0_xattn_bk, L0_xattn_Wv, L0_xattn_bv,
           L0_xattn_Wo, L0_xattn_bo, L0_ffn_waff, L0_ffn_W1, L0_ffn_b1, L0_ffn_W2, L0_ffn_b2, L0_ffn_affinity_threshold,
           L1_xattn_ln1_s, L1_xattn_ln1_b, L1_xattn_lnc_s, L1_xattn_lnc_b, L1_xattn_Wq, L1_xattn_Wkv, L1_xattn_null_kv,
           L1_xattn_Wo, L1_xattn_lno_s, L1_xattn_lno_b, L1_ffn_w_gate, L1_ffn_w_up, L1_ffn_w_down):
    import numpy as np
    import concourse.bacc as bacc
    from concourse.bass_utils import run_bass_kernel_spmd

    def T(a):
        return np.ascontiguousarray(np.swapaxes(np.asarray(a), -1, -2))

    def plain(a):
        return np.ascontiguousarray(np.asarray(a))

    H, inner = 16, L1_xattn_Wq.shape[1]
    B, S, D = x.shape
    E, F = L0_ffn_b1.shape
    mask = plain(mask_BxS2_bf1).view(np.uint8)
    parts, sel = np.zeros((P, 4), np.float32), np.zeros((P, H), np.float32)
    for column, rows in ((0, (0, 64, 96)), (1, (16, 80)), (2, (32,)), (3, (0, 64, 96))):
        for r in rows:
            parts[r:r + H, column] = 1
    sel[np.arange(P), np.arange(P) % H] = 1
    arrays = dict(
        x=plain(x), ctx=plain(ctx_1024), ctxT=T(ctx_1024),
        L0_Wq=T(L0_xattn_Wq), L0_Wk=T(L0_xattn_Wk), L0_Wv=T(L0_xattn_Wv), L0_Wo=T(L0_xattn_Wo),
        L0_bq=plain(L0_xattn_bq), L0_bk=plain(L0_xattn_bk), L0_bv=plain(L0_xattn_bv), L0_bo=plain(L0_xattn_bo),
        E_W1=plain(L0_ffn_W1), E_W2=plain(L0_ffn_W2), E_b1=plain(L0_ffn_b1), E_b2=plain(L0_ffn_b2),
        E_b1T=T(plain(L0_ffn_b1).reshape(E * F // P, P)), E_waffT=T(L0_ffn_waff),
        E_thr=plain(L0_ffn_affinity_threshold).reshape(1),
        E_tile_no=np.arange(B + E, dtype=np.float32).reshape(1, B + E),
        A_WqT=T(L1_xattn_Wq), A_WkT=T(plain(L1_xattn_Wkv)[:, :inner]), A_Wkv=plain(L1_xattn_Wkv), A_Wo=plain(L1_xattn_Wo),
        A_ln1_s=plain(L1_xattn_ln1_s), A_ln1_b=plain(L1_xattn_ln1_b), A_lnc_s=plain(L1_xattn_lnc_s),
        A_lnc_b=plain(L1_xattn_lnc_b), A_lno_s=plain(L1_xattn_lno_s), A_lno_b=plain(L1_xattn_lno_b),
        A_null_kv=plain(L1_xattn_null_kv), A_mask=mask, A_maskT=T(mask), A_parts=parts, A_sel=sel,
        A_eps2=np.tile(np.array([[EPS_BLOCK, EPS_L1]], np.float32), (P, 1)),
        F_gateT=T(L1_ffn_w_gate), F_upT=T(L1_ffn_w_up), F_downT=T(L1_ffn_w_down),
    )
    nc = bacc.Bacc("TRN2", target_bir_lowering=False, num_devices=1)
    d = {n: nc.dram_tensor("in_" + n, a.shape, mybir.dt.from_np(a.dtype), kind="ExternalInput").ap() for n, a in arrays.items()}
    out = nc.dram_tensor("out", (B, S, D), F32, kind="ExternalOutput").ap()
    two_layers(nc, d, out)
    r = run_bass_kernel_spmd(nc, [{"in_" + n: a for n, a in arrays.items()}], core_ids=[0])
    return r.results[0]["out"]
```
